# Optimizing a Trainium2 kernel written in Bass

```python
import numpy as np
import jax
import jax.numpy as jnp

def _softmax(x, axis=-1):
    return jax.nn.softmax(x, axis=axis)

def _gelu(x):
    return jax.nn.gelu(x, approximate=True)

def _silu(x):
    return jax.nn.silu(x)

def _sigmoid(x):
    return jax.nn.sigmoid(x)

def _layernorm(x, axis=-1, eps=1e-05):
    m = jnp.mean(x, axis=axis, keepdims=True)
    v = jnp.var(x, axis=axis, keepdims=True)
    return (x - m) / jnp.sqrt(v + eps)

def _scatter_add(tgt, idx, src, axis=0):
    return tgt.at[idx].add(src)

def _segment_sum(src, seg, n):
    return jax.ops.segment_sum(src, seg, n)
kernel_name = 'mk_gnn_resnorm_d2_gnn_r32_a4d7d7'

def setup_inputs(seed: int=0):
    np.random.seed(seed)
    _w = jnp.asarray

    def _rec_inputs():
        import jax
        import jax.numpy as jnp
        _gk = jax.random.key(seed)
        x = -0.0003713 + 1 * jax.random.normal(jax.random.fold_in(_gk, 1), (3125, 256), jnp.float32)
        _s = jax.random.randint(jax.random.fold_in(_gk, 2), (25000,), 0, 3125, jnp.int32)
        _d = jax.random.randint(jax.random.fold_in(_gk, 3), (25000,), 0, 3125, jnp.int32)
        _loop = jnp.arange(3125, dtype=jnp.int32)
        src = jnp.concatenate([_s, _d, _loop])
        dst = jnp.concatenate([_d, _s, _loop])
        _o = jnp.argsort(dst, stable=True)
        src = src[_o]
        dst = dst[_o]
        edge_attr_3 = -1.09012e-05 + 0.99985 * jax.random.normal(jax.random.fold_in(_gk, 11), (53125, 3), jnp.float32)
        return (x, src, dst, edge_attr_3)
    x, src, dst, edge_attr_3 = _rec_inputs()

    def _L0_gnn_setup():
        import jax, jax.numpy as jnp
        import numpy as np
        N = 50000
        E = 25000
        F_DIM = 256
        H = 4
        C = 64
        SLOPE = 0.2

        def gat_layer(x, src, dst, W, a_src, a_dst, bias, heads, out_ch):
            n = x.shape[0]
            xW = (x @ W).reshape(n, heads, out_ch)
            alpha_s = jnp.sum(xW * a_src, axis=-1)
            alpha_d = jnp.sum(xW * a_dst, axis=-1)
            e = jax.nn.leaky_relu(alpha_s[src] + alpha_d[dst], SLOPE)
            m = jax.ops.segment_max(e, dst, num_segments=n)
            w = jnp.exp(e - m[dst])
            z = jax.ops.segment_sum(w, dst, num_segments=n)
            alpha = w / z[dst]
            out = jax.ops.segment_sum(xW[src] * alpha[:, :, None], dst, num_segments=n)
            return out.reshape(n, heads * out_ch) + bias
        key = jax.random.key(seed)
        ks = jax.random.split(key, 11)
        s = 0.05
        return {'x': jax.random.normal(ks[0], (N, F_DIM), jnp.float32), 'edge_index': jax.random.randint(ks[1], (2, E), 0, N), 'W1': jax.random.normal(ks[2], (F_DIM, H * C), jnp.float32) * s, 'a_src1': jax.random.normal(ks[3], (H, C), jnp.float32) * s, 'a_dst1': jax.random.normal(ks[4], (H, C), jnp.float32) * s, 'b1': jnp.zeros((H * C,), jnp.float32), 'W2': jax.random.normal(ks[5], (H * C, F_DIM), jnp.float32) * s, 'a_src2': jax.random.normal(ks[6], (1, F_DIM), jnp.float32) * s, 'a_dst2': jax.random.normal(ks[7], (1, F_DIM), jnp.float32) * s, 'b2': jnp.zeros((F_DIM,), jnp.float32)}
    _L0_gnn_all = _L0_gnn_setup()
    _L0_gnn_in = {k: v for k, v in _L0_gnn_all.items() if k in ('W1', 'a_src1', 'a_dst1', 'b1', 'W2', 'a_src2', 'a_dst2', 'b2')}
    del _L0_gnn_all

    def _L1_gnn_setup():
        import jax, jax.numpy as jnp
        import numpy as np
        N = 50000
        E = 12500
        IN = 256
        H = 8
        D = 32
        EF = 3
        key = jax.random.key(seed)
        ks = jax.random.split(key, 8)
        x = jax.random.normal(ks[0], (N, IN), dtype=jnp.float32)
        edge_index = jax.random.randint(ks[1], (2, E), 0, N, dtype=jnp.int64)
        edge_attr = jax.random.normal(ks[2], (E, EF), dtype=jnp.float32)
        W = jax.random.normal(ks[3], (H * D, IN), dtype=jnp.float32) * np.float32(np.sqrt(2.0 / (IN + H * D)))
        a_src = jax.random.normal(ks[4], (H, D), dtype=jnp.float32) * np.float32(np.sqrt(2.0 / (H + D)))
        a_dst = jax.random.normal(ks[5], (H, D), dtype=jnp.float32) * np.float32(np.sqrt(2.0 / (H + D)))
        edge_W = jax.random.normal(ks[6], (H * D, EF), dtype=jnp.float32) * np.float32(np.sqrt(2.0 / (EF + H * D)))
        edge_b = jnp.zeros((H * D,), dtype=jnp.float32)
        bias = jnp.zeros((H * D,), dtype=jnp.float32)
        return {'x': x, 'W': W, 'a_src': a_src, 'a_dst': a_dst, 'edge_W': edge_W, 'edge_b': edge_b, 'bias': bias, 'edge_attr': edge_attr, 'edge_index': edge_index}
    _L1_gnn_all = _L1_gnn_setup()
    _L1_gnn_in = {k: v for k, v in _L1_gnn_all.items() if k in ('W', 'a_src', 'a_dst', 'edge_W', 'edge_b', 'bias')}
    del _L1_gnn_all
    return {'x': x, 'src': src, 'dst': dst, 'edge_attr_3': edge_attr_3, 'L0_gnn_W1': _L0_gnn_in['W1'], 'L0_gnn_a_src1': _L0_gnn_in['a_src1'], 'L0_gnn_a_dst1': _L0_gnn_in['a_dst1'], 'L0_gnn_b1': _L0_gnn_in['b1'], 'L0_gnn_W2': _L0_gnn_in['W2'], 'L0_gnn_a_src2': _L0_gnn_in['a_src2'], 'L0_gnn_a_dst2': _L0_gnn_in['a_dst2'], 'L0_gnn_b2': _L0_gnn_in['b2'], 'L1_gnn_W': _L1_gnn_in['W'], 'L1_gnn_a_src': _L1_gnn_in['a_src'], 'L1_gnn_a_dst': _L1_gnn_in['a_dst'], 'L1_gnn_edge_W': _L1_gnn_in['edge_W'], 'L1_gnn_edge_b': _L1_gnn_in['edge_b'], 'L1_gnn_bias': _L1_gnn_in['bias']}

def reference(x, src, dst, edge_attr_3, L0_gnn_W1, L0_gnn_a_src1, L0_gnn_a_dst1, L0_gnn_b1, L0_gnn_W2, L0_gnn_a_src2, L0_gnn_a_dst2, L0_gnn_b2, L1_gnn_W, L1_gnn_a_src, L1_gnn_a_dst, L1_gnn_edge_W, L1_gnn_edge_b, L1_gnn_bias):
    import jax
    import jax.numpy as jnp

    def _L0_gnn_ref(x, edge_index, W1, a_src1, a_dst1, b1, W2, a_src2, a_dst2, b2):
        import jax, jax.numpy as jnp
        import numpy as np
        N = 50000
        E = 25000
        F_DIM = 256
        H = 4
        C = 64
        SLOPE = 0.2

        def gat_layer(x, src, dst, W, a_src, a_dst, bias, heads, out_ch):
            n = x.shape[0]
            xW = (x @ W).reshape(n, heads, out_ch)
            alpha_s = jnp.sum(xW * a_src, axis=-1)
            alpha_d = jnp.sum(xW * a_dst, axis=-1)
            e = jax.nn.leaky_relu(alpha_s[src] + alpha_d[dst], SLOPE)
            m = jax.ops.segment_max(e, dst, num_segments=n)
            w = jnp.exp(e - m[dst])
            z = jax.ops.segment_sum(w, dst, num_segments=n)
            alpha = w / z[dst]
            out = jax.ops.segment_sum(xW[src] * alpha[:, :, None], dst, num_segments=n)
            return out.reshape(n, heads * out_ch) + bias
        loop = jnp.arange(N)
        src = jnp.concatenate([edge_index[0], loop])
        dst = jnp.concatenate([edge_index[1], loop])
        h = jax.nn.elu(gat_layer(x, src, dst, W1, a_src1, a_dst1, b1, H, C))
        return gat_layer(h, src, dst, W2, a_src2, a_dst2, b2, 1, F_DIM)

    def _L1_gnn_ref(x, W, a_src, a_dst, edge_W, edge_b, bias, edge_attr, edge_index):
        import jax, jax.numpy as jnp
        import numpy as np
        N = 50000
        E = 12500
        IN = 256
        H = 8
        D = 32
        EF = 3
        n = x.shape[0]
        h = (x @ W.T).reshape(n, H, D)
        src, dst = (edge_index[0], edge_index[1])
        h_src = h[src]
        h_dst = h[dst]
        alpha = jnp.einsum('ehd,hd->eh', h_src, a_src) + jnp.einsum('ehd,hd->eh', h_dst, a_dst)
        enc = jax.nn.relu(edge_attr @ edge_W.T + edge_b).reshape(-1, H, D)
        alpha = alpha + jnp.sum(enc * h_dst, axis=-1)
        alpha = jnp.where(alpha >= 0, alpha, 0.2 * alpha)
        amax = jax.ops.segment_max(alpha, dst, num_segments=n)
        ex = jnp.exp(alpha - amax[dst])
        denom = jax.ops.segment_sum(ex, dst, num_segments=n)
        attn = ex / jnp.maximum(denom[dst], 1e-10)
        out = jax.ops.segment_sum(h_src * attn[..., None], dst, num_segments=n)
        return out.reshape(n, H * D) + bias
    edge_index = jnp.stack([src, dst])
    x = _layernorm(x + _L0_gnn_ref(x, edge_index, L0_gnn_W1, L0_gnn_a_src1, L0_gnn_a_dst1, L0_gnn_b1, L0_gnn_W2, L0_gnn_a_src2, L0_gnn_a_dst2, L0_gnn_b2), axis=-1)
    x = _layernorm(x + _L1_gnn_ref(x, L1_gnn_W, L1_gnn_a_src, L1_gnn_a_dst, L1_gnn_edge_W, L1_gnn_edge_b, L1_gnn_bias, edge_attr_3, edge_index), axis=-1)
    return x

_drawn_inputs = setup_inputs


def setup_inputs(seed=0):
    import zlib

    import numpy as np

    out = dict(_drawn_inputs(seed))
    spreads = {'L0_gnn_b1': (0.0, 0.1),
     'L0_gnn_b2': (0.0, 0.1),
     'L1_gnn_edge_b': (0.0, 0.1),
     'L1_gnn_bias': (0.0, 0.1)}
    factors = {'L0_gnn_a_src1': 2.816, 'L0_gnn_a_dst1': 8.0, 'L0_gnn_a_src2': 8.0, 'L0_gnn_a_dst2': 31.93}
    for name, (base, spread) in spreads.items():
        noise = np.random.default_rng([zlib.crc32(name.encode()), seed]).standard_normal(out[name].shape)
        drawn = base * np.exp(spread * noise) if base else spread * noise
        out[name] = jnp.asarray(drawn.astype(out[name].dtype))
    for name, factor in factors.items():
        out[name] = (out[name] * factor).astype(out[name].dtype)
    return out
```

```python
from contextlib import ExitStack

import concourse.bass as bass
from concourse import mybir

F32 = mybir.dt.float32
I32 = mybir.dt.int32
ALU = mybir.AluOpType
ACT = mybir.ActivationFunctionType
AX = mybir.AxisListType

P = 128
N = 3125
D = 256
E = 53125
BLOCKS = -(-N // P)
FULL = N // P
REST = N - FULL * P
TILES = -(-E // P)
SLOTS = TILES + BLOCKS - 1
B = 11
K = SLOTS // B
BPAD = 12
Q = SLOTS // 4
BIG = 1.0e30
RING = 3
EPS = 1e-5
SLOPE = 0.2
SEED = 4
ENC_AT = 2
assert SLOTS == B * K and SLOTS == 4 * Q and Q <= P

HEADS = (4, 1, 8)
CH = tuple(D // h for h in HEADS)
COLS = (CH[0] + 2, CH[1] + 2, CH[2] + 1)
VALS = tuple(h * c for h, c in zip(HEADS, COLS))
ROW = tuple(v + h for v, h in zip(VALS, HEADS))
VMAX, RMAX = max(VALS), max(ROW)
SELF = (True, True, False)
META = tuple(h + 3 + (not s) for h, s in zip(HEADS, SELF))

PEN_F, PEN_B, PEN_L, PEN_R, START = range(5)


class Batch:

    def __init__(self, j, u):
        self.j, self.u = (j + u // RING), u % RING
        self.k = self.j * RING + self.u

    def after(self, n):
        return Batch(self.j, self.u + n)


def gat_kernel(nc, x, src, dst, edge_attr, w1, as1, ad1, b1, w2, as2, ad2, b2, w3, as3, ad3, edge_w, edge_b, b3, out):
    ctx = ExitStack()
    with ctx:
        def sb(name, shape, dt=F32):
            return ctx.enter_context(nc.sbuf_tensor(name, shape, dt))

        def dram(name, shape, dt=F32):
            return nc.dram_tensor(name, shape, dt, kind="Internal").ap()

        def sem(name):
            return ctx.enter_context(nc.semaphore(name))

        dst_pad = dram("dst_pad", (TILES * P,), I32)
        src_pad = dram("src_pad", (TILES * P,), I32)
        attr_pad = dram("attr_pad", (TILES * P * 3,))
        keys_d = dram("keys_d", (SLOTS * P + 2,))
        flags_d = dram("flags_d", (SLOTS, 5 * P))
        chain_d = dram("chain_d", (2, SLOTS))
        carry_d = dram("carry_d", (SLOTS, 2, P))
        index_d = dram("index_d", (K, P, B), I32)
        attrT_d = dram("attrT_d", (3, SLOTS * P))
        table = [dram(f"table{l}", (BLOCKS * P, ROW[l])) for l in range(3)]

        nodes = sb("nodes", [P, BLOCKS, D])
        sums = sb("sums", [P, BLOCKS * VMAX])
        late = sb("late", [P, BLOCKS * D + RING * B * P])
        rows = sb("rows", [P, RING, B, RMAX])
        onehot = sb("onehot", [P, RING, B, P])
        onehotT = sb("onehotT", [P, RING, B, P])
        flags = sb("flags", [8 * B, RING, 5, P])
        chain = sb("chain", [1, RING, 2, 8, B + 1])
        carry = sb("carry", [2, RING, P])
        index = sb("index", [P, RING, B], I32)
        loc = sb("loc", [P, SLOTS])
        blk = sb("blk", [1, K * BPAD], I32)
        dtab = sb("dtab", [P, BLOCKS, 8])
        score = sb("score", [P, 2, 8 * B])
        scoreT = sb("scoreT", [8 * B, 2, P])
        top = sb("top", [8 * B, 3, P])
        seg = sb("seg", [8 * B, P])
        expT = sb("expT", [8 * B, 2, P])
        ends = sb("ends", [1, 2, 8 * (B + 1)])
        runs = sb("runs", [1, 2, 8 * (B + 1)])
        linkrow = sb("linkrow", [1, 2, 8 * B])
        newtop = sb("newtop", [1, 8])
        drop = sb("drop", [1, 8])
        scale = sb("scale", [2, 8])
        wgt = sb("wgt", [P, RING, 8 * B])
        enc = sb("enc", [P, 3, D])
        prod = sb("prod", [P, 3, D])
        dots = sb("dots", [P, RING, B, 8])
        wts = [sb(f"wts{l}", [P, 2, D + 2 * HEADS[l]]) for l in range(3)]
        avec = sb("avec", [P, 2, D])
        bias = sb("bias", [P, 3, D])
        edgew = sb("edgew", [4, D])
        ident = sb("ident", [P, P])
        iota = sb("iota", [P, P])
        ones = sb("ones", [P, 1])
        zeros = sb("zeros", [P, VMAX])
        flat = rows[:, :, :, :].rearrange("p r s c -> p (r s c)")
        at = [0]

        def tile(*shape):
            n = 1
            for d in shape:
                n *= d
            at[0] += n
            t = flat[:, at[0] - n:at[0]]
            return t.rearrange("p (u c) -> p u c", u=shape[0]) if len(shape) == 2 else t.rearrange(
                "p (u c n) -> p u c n", u=shape[0], c=shape[1])
        yin, yT, trow = tile(2, D), tile(2, 2, P), tile(2, RMAX)
        self_row, work = tile(2, VMAX), tile(2, VMAX)
        work2, work3, expo = tile(2, D), tile(2, D), tile(2, D)
        small = sb("small", [P, 2, 4, 8])
        stats = sb("stats", [P, 2, 6])
        mv = sb("mv", [P, 2, 2])
        meanvar = sb("meanvar", [P, BLOCKS, 2])
        rstd = sb("rstd", [P, BLOCKS])

        hnode = late[:, 0:BLOCKS * D].rearrange("p (b f) -> p b f", b=BLOCKS)
        attrT = late[0:4, BLOCKS * D:].rearrange("p (r f) -> p r f", r=RING)

        def part(at, n, p=Q):
            return late[0:p, at:at + n]
        flg = part(0, 4 * 5 * P).rearrange("p (c t e) -> p c t e", c=4, t=5)
        attr_g = part(2560, 1536).rearrange("p (c e j) -> p c e j", c=4, j=3)
        attr_t = part(4096, 1536).rearrange("p (c j e) -> p c j e", c=4, j=3)
        car = part(5632, 512).rearrange("p (c e) -> p c e", c=4)
        dst_g = part(6144, 512).bitcast(I32)
        src_g = part(6656, 512).bitcast(I32)
        dstf, srcf, loc_g, key, kprev, knext = (
            part(7168 + 512 * i, 512).rearrange("p (c e) -> p c e", c=4) for i in range(6))
        dst_all = sums[:, 0:TILES].bitcast(I32)
        dst_allf = sums[:, TILES:2 * TILES]
        dead = sums[:, 2 * TILES:3 * TILES]
        slot_gt = sums[0:BLOCKS - 1, 1248:1248 + K * BPAD]
        slot_gt2 = sums[0:BLOCKS - 1, 1728:1728 + SLOTS]
        siota = sums[0:BLOCKS - 1, 2168:2168 + K * BPAD]
        siota2 = sums[0:BLOCKS - 1, 2648:2648 + SLOTS]
        counts = sums[:, 3088:3088 + BLOCKS - 1]
        misc = sums[:, 3120:3200]
        guard = sums[0:1, 3200:3202]
        tail_i = sums[0:1, 3300:3300 + 2 * P].bitcast(I32)
        tail_f = sums[0:1, 3600:3600 + 3 * P]
        index_all = sums[:, 5200:5200 + SLOTS].bitcast(I32)
        car1 = sums[0:Q, 5700:6212].rearrange("p (c e) -> p c e", c=4)
        w3in = sums[:, 4000:4000 + 2 * D].rearrange("p (c n) -> p c n", c=2)
        wprod = sums[:, 4600:4600 + 2 * D].rearrange("p (c n) -> p c n", c=2)

        bank = [ctx.enter_context(nc.psum_tensor(f"bank{i}", [P, 512], F32)) for i in range(8)]
        ps_hot, ps_T, ps_e = bank[0], bank[1], bank[2]
        AD, WT, QT, FAC = 0, 96, 192, 288
        ps_row = ps_T[0:1, 256:256 + 2 * 8 * B]
        ps_col = ps_T[0:8 * B, 440:442]
        ps_sum = ([bank[i] for i in (3, 4, 5, 6)], [bank[i] for i in (3, 4, 5, 6)], [bank[i] for i in (3, 4)])
        ps_enc = [bank[i] for i in (5, 6, 7)]
        ps_yT = [bank[i] for i in (3, 4)]
        ps_y = [bank[i] for i in (5, 6)]

        names = ("hot hotp hotT ad sc1 sc2 sc scp scT top0 topf top endp ends0 ends1 ends2 runl runr link rnew rdrop rscale "
                 "fac col seg1 seg diff exp mask wp w resc mul agg add encp enc prod dot "
                 "ycopy yTp yT yp tval tas tad tself0 tself tclear e1 e2 e3 e4 e5 e6 e7 e8 ex st1 st2 agr norm").split()
        ev = {n: sem("ev_" + n) for n in names}
        s_passed = {}
        s_in = sem("s_in")
        s_pad = sem("s_pad")
        s_w = sem("s_w")
        s_avec = sem("s_avec")
        s_dst = sem("s_dst")
        s_got = sem("s_got")
        s_key = sem("s_key")
        s_near = sem("s_near")
        s_flag = sem("s_flag")
        p_pool, p_dve, p_pe, p_act = sem("p_pool"), sem("p_dve"), sem("p_pe"), sem("p_act")
        s_layer = sem("s_layer")
        s_index = [[sem(f"s_index{l}_{u}") for u in range(RING)] for l in range(3)]
        s_meta = [[sem(f"s_meta{l}_{u}") for u in range(RING)] for l in range(3)]
        s_rows = [[sem(f"s_rows{l}_{u}") for u in range(RING)] for l in range(3)]
        s_tab = [[sem(f"s_tab{l}_{u}") for u in range(2)] for l in range(3)]
        s_self = [[sem(f"s_self{l}_{u}") for u in range(2)] for l in range(2)]
        s_out = sem("s_out")

        def need(eng, name, count):
            if isinstance(count, int) and count <= 0:
                return
            eng.wait_ge(ev[name], count + SEED)

        def need_apart(eng, *waits):
            for w, c in waits:
                if isinstance(w, str):
                    need(eng, w, c)
                else:
                    eng.wait_ge(w, c)
                if not isinstance(c, int):
                    eng.sem_inc(s_passed[eng], 1)

        def seeded(eng, which):
            for n in which.split():
                eng.sem_inc(ev[n], SEED)

        def done(inst, name):
            return inst.then_inc(ev[name], 1)

        def free(eng, s, b, u):
            if not isinstance(b, int) or b > 1:
                eng.wait_ge(s, (b - u) * 8)

        def pairs(eng, body):
            body(0, 0)
            body(1, 1)
            with eng.Fori(1, BLOCKS // 2) as j:
                body(j * 2, 0)
                body(j * 2 + 1, 1)
            body(BLOCKS - 1, 0)

        def batches(eng, body, load):
            loops = (K - 3) // RING
            with eng.Fori(0, loops) as j:
                for u in range(RING):
                    load(Batch(j, u))
                    body(Batch(j, u), K)
            for k in range(loops * RING, K):
                load(Batch(k // RING, k % RING))
                body(Batch(k // RING, k % RING), K - k)

        def block_regs(eng, tag):
            return [eng.alloc_register(f"{tag}{i}") for i in range(B)]

        MARKS = {}
        block = ctx.enter_context(nc.Block())

        @block.vector
        def _(dve):
            s_passed[dve] = sem("s_passed_dve")
            v = nc.vector
            seeded(dve, "hot sc1 sc2 sc top0 topf top ends0 ends1 ends2 runl runr rnew rdrop seg1 seg diff mask "
                        "resc mul add prod dot tas tad tself0 tself e1 e4 e5 e6 e7 e8 st1 st2 agr norm")
            regs = block_regs(dve, "blk_dve")
            step = [0]

            def ch(inst):
                step[0] += 1
                inst.then_inc(p_dve, 1)
                dve.wait_ge(p_dve, step[0])
                return step[0]

            def mark(name):
                MARKS[name] = step[0]

            def ones_cols(l):
                H, V, C = HEADS[l], COLS[l], CH[l]
                for u in range(2):
                    ch(v.memset(trow[:, u, 0:H * V].rearrange("p (h c) -> p h c", h=H)[:, :, C:V], 1.0))
            ones_cols(0)
            mark("ONES_DONE")
            dve.wait_ge(s_dst, 16)
            ch(v.tensor_copy(dst_allf, dst_all))
            for b in range(1, BLOCKS):
                ch(v.tensor_scalar(dead, dst_allf, float(P * b), 0.0, ALU.is_lt, ALU.add,
                                   accum_out=counts[:, b - 1:b]))
            mark("COUNT_DONE")
            dve.wait_ge(p_pe, 1)
            dve.wait_ge(p_pool, 13)
            off = misc[0:BLOCKS - 1, 1:2].bitcast(I32)
            shl = misc[0:BLOCKS - 1, 2:3].bitcast(I32)
            pos = misc[0:BLOCKS - 1, 3:4]
            ch(v.tensor_copy(off, ps_e[0:BLOCKS - 1, 0:1]))
            ch(v.tensor_scalar(shl, off, 7, None, ALU.logical_shift_right))
            ch(v.tensor_copy(pos, shl))
            ch(v.tensor_tensor(pos, pos, misc[0:BLOCKS - 1, 0:1], ALU.add))
            ch(v.tensor_scalar(slot_gt, siota, pos, None, ALU.is_gt))
            ch(v.tensor_scalar(slot_gt2, siota2, pos, None, ALU.is_gt))
            mark("GT_DONE")
            dve.wait_ge(p_pe, 6)
            ch(v.tensor_copy(blk[:, :], ps_T[0:1, 0:K * BPAD]))
            bcol = misc[0:Q, 8:12]
            b128 = misc[0:Q, 12:16]
            ch(v.tensor_copy(bcol, ps_hot[0:Q, 0:4]))
            ch(v.tensor_scalar(b128, bcol, float(P), None, ALU.mult))
            ch(v.tensor_tensor(misc[0:Q, 16:20].bitcast(I32), misc[0:Q, 4:8], bcol, ALU.subtract))
            mark("TILE_DONE")
            dve.wait_ge(s_got, 16 * 12)
            ch(v.tensor_copy(dstf.rearrange("p c e -> p (c e)"), dst_g))
            ch(v.tensor_copy(srcf.rearrange("p c e -> p (c e)"), src_g))
            for c in range(4):
                ch(v.tensor_scalar(loc_g[:, c, :], dstf[:, c, :], b128[:, c:c + 1], None, ALU.subtract))
            mark("LOC_DONE")
            ch(v.tensor_scalar(key, loc_g, float(P), None, ALU.is_lt))
            ch(v.scalar_tensor_tensor(key, loc_g, 0.0, key, ALU.is_ge, ALU.mult))
            ch(v.scalar_tensor_tensor(key, dstf, 1.0, key, ALU.add, ALU.mult))
            ch(v.tensor_scalar(key, key, -1.0, None, ALU.add))
            mark("KEY_DONE")
            ch(v.tensor_copy(attr_t, attr_g.rearrange("p c e j -> p c j e")))
            dve.wait_ge(p_pe, 14)
            ch(v.tensor_copy(loc[:, :], bank[3][:, 0:SLOTS]))
            ch(v.tensor_copy(index_all, bank[4][:, 0:SLOTS]))
            dve.wait_ge(s_w, 16 * 8)
            def products(l):
                H, C = HEADS[l], CH[l]
                dve.wait_ge(s_avec, 32 * (l + 1))
                for i in range(2):
                    ch(v.tensor_tensor(wprod, wts[l][:, :, 0:D], avec[:, i, :].unsqueeze(1).to_broadcast([P, 2, D]),
                                       ALU.mult))
                    ch(v.tensor_reduce(wts[l][:, :, D + i * H:D + (i + 1) * H],
                                       wprod.rearrange("p c (h n) -> p c h n", h=H), AX.X, ALU.add))
            products(0)
            mark("AVEC0")
            products(1)
            mark("AVEC1")
            dve.wait_ge(p_pe, 18)
            for c in range(2):
                ch(v.tensor_copy(wts[2][:, c, 0:D], bank[5][:, c * D:(c + 1) * D]))
            products(2)
            mark("WA_DONE")
            dve.wait_ge(s_near, 32)
            ch(v.tensor_tensor(flg[:, :, START, :], key, kprev, ALU.not_equal))
            ch(v.tensor_scalar(flg[:, :, PEN_F, :], flg[:, :, START, :], -BIG, None, ALU.mult))
            ch(v.tensor_tensor(flg[:, :, PEN_B, :], key, knext, ALU.not_equal))
            ch(v.tensor_scalar(flg[:, :, PEN_B, :], flg[:, :, PEN_B, :], -BIG, None, ALU.mult))
            for c in range(4):
                ch(v.tensor_scalar(flg[:, c, PEN_L, :], key[:, c, :], kprev[:, c, 0:1], -BIG,
                                   ALU.not_equal, ALU.mult))
                ch(v.tensor_scalar(flg[:, c, PEN_R, :], key[:, c, :], knext[:, c, P - 1:P], -BIG,
                                   ALU.not_equal, ALU.mult))
            one, cl, cr = misc[0:Q, 20:24], misc[0:Q, 24:28], misc[0:Q, 28:32]
            pab = misc[0:Q, 40:48].rearrange("p (t c) -> p t c", t=2)
            ch(v.tensor_tensor(one, key[:, :, 0], key[:, :, P - 1], ALU.is_equal))
            ch(v.tensor_tensor(cl, key[:, :, 0], kprev[:, :, 0], ALU.is_equal))
            ch(v.tensor_tensor(cr, key[:, :, P - 1], knext[:, :, P - 1], ALU.is_equal))
            for c in range(4):
                ch(v.tensor_scalar(car[:, c, :], iota[0:Q, :], loc_g[:, c, 0:1], cl[:, c:c + 1],
                                   ALU.is_equal, ALU.mult))
            ch(v.tensor_scalar(car1, car, -1.0, 1.0, ALU.mult, ALU.add))
            for i, w in enumerate((cl, cr)):
                ch(v.tensor_tensor(pab[:, i, :], w, one, ALU.mult))
                ch(v.tensor_scalar(pab[:, i, :], pab[:, i, :], -1.0, BIG, ALU.add, ALU.mult))
            mark("PREP_DONE")

            for l in range(3):
                H, C, V, VV = HEADS[l], CH[l], COLS[l], VALS[l]
                base = l * BLOCKS
                if l:
                    need(dve, "add", l * K * B)
                    for u in range(2):
                        dve.wait_ge(s_tab[l - 1][u], 16 * ((BLOCKS + 1 - u) // 2))
                    ones_cols(l)

                def epilogue0(b, u):
                    Hh, Vh, W = HEADS[0], COLS[0], VALS[0]
                    a = sums[:, bass.ds(b * W, W)].rearrange("p (h c) -> p h c", h=Hh)
                    need(dve, "e2", b - 1)
                    done(v.scalar_tensor_tensor(small[:, u, 0, 0:Hh], a[:, :, Vh - 2], 0.0, a[:, :, Vh - 1],
                                                ALU.is_equal, ALU.add), "e1")
                    need(dve, "e3", b + 1)
                    t = work[:, u, 0:W].rearrange("p (h c) -> p h c", h=Hh)
                    done(v.reciprocal(small[:, u, 1, 0:Hh], t[:, :, Vh - 2]), "e4")
                    need(dve, "e4", b + 1)
                    done(v.tensor_tensor(work2[:, u, :].rearrange("p (h c) -> p h c", h=Hh), t[:, :, 0:CH[0]],
                                         small[:, u, 1, 0:Hh].unsqueeze(2).to_broadcast([P, Hh, CH[0]]),
                                         ALU.mult), "e5")
                    need(dve, "e5", b + 1)
                    done(v.tensor_tensor(work2[:, u, :], work2[:, u, :], bias[:, 0, :], ALU.add), "e6")
                    need(dve, "e6", b + 1)
                    need(dve, "ex", b - 1)
                    done(v.tensor_scalar(work3[:, u, :], work2[:, u, :], 0.0, None, ALU.min), "e7")
                    done(v.tensor_scalar(work2[:, u, :], work2[:, u, :], 0.0, -1.0, ALU.max, ALU.add), "st1")
                    need(dve, "st1", b + 1)
                    need(dve, "ex", b + 1)
                    need(dve, "yTp", BLOCKS + b - 1)
                    done(v.tensor_tensor(yin[:, u, :], work2[:, u, :], expo[:, u, :], ALU.add), "e8")

                def scores_out(b, u, l=l, H=H, VV=VV, base=base):
                    need(dve, "tval", base + b + 1)
                    free(dve, s_tab[l][u], b, u)
                    done(v.tensor_copy(trow[:, u, VV:VV + H], ps_y[u][:, D:D + H]), "tas")
                    d = dtab[:, bass.ds(b, 1), :].rearrange("p a n -> p (a n)")
                    done(v.tensor_copy(d[:, 0:H], ps_y[u][:, D + H:D + 2 * H]), "tad")
                    if SELF[l]:
                        need(dve, "tas", base + b + 1)
                        need(dve, "tad", base + b + 1)
                        t = small[:, u, 2, 0:H]
                        done(v.tensor_tensor(t, trow[:, u, VV:VV + H], d[:, 0:H], ALU.add), "tself0")
                        need(dve, "tself0", base + b + 1)
                        done(v.scalar_tensor_tensor(d[:, H:2 * H], t, SLOPE, t, ALU.mult, ALU.max), "tself")

                def epilogue1(b, u):
                    W = VALS[1]
                    a = sums[:, bass.ds(b * W, W)]
                    i = BLOCKS + b
                    done(v.scalar_tensor_tensor(small[:, u, 0, 0:1], a[:, D:D + 1], 0.0, a[:, D + 1:D + 2],
                                                ALU.is_equal, ALU.add), "e1")
                    need(dve, "e1", i + 1)
                    dve.wait_ge(s_self[1][u], (b - u) * 8 + 16)
                    v.scalar_tensor_tensor(work[:, u, 0:D + 1], self_row[:, u, 0:D + 1], small[:, u, 0, 0:1],
                                           a[:, 0:D + 1], ALU.mult, ALU.add).then_inc(ev["e2"], 1)
                    need(dve, "e2", i + 1)
                    done(v.reciprocal(small[:, u, 1, 0:1], work[:, u, D:D + 1]), "e4")
                    need(dve, "e4", i + 1)
                    done(v.scalar_tensor_tensor(work2[:, u, :], work[:, u, 0:D], small[:, u, 1, 0:1], bias[:, 1, :],
                                                ALU.mult, ALU.add), "e5")
                    need(dve, "e5", i + 1)
                    y = nodes[:, bass.ds(b, 1), :].rearrange("p a f -> p (a f)")
                    done(v.tensor_tensor(y, y, work2[:, u, :], ALU.add), "e6")
                    need_apart(dve, ("e6", i + 1))
                    done(v.bn_stats(stats[:, u, :], y), "st2")
                    need_apart(dve, ("st2", b + 1))
                    done(v.bn_aggr(mv[:, u, :], stats[:, u, :]), "agr")
                    need(dve, "agr", b + 1)
                    done(v.tensor_copy(meanvar[:, bass.ds(b, 1), :].rearrange("p a f -> p (a f)"), mv[:, u, :]), "st1")

                def normalise(n, l_):
                    if l_ == 1:
                        need(dve, "st1", 2 * BLOCKS)
                    else:
                        need(dve, "st1", 3 * BLOCKS)
                    ch(v.tensor_scalar(meanvar[:, :, 1], meanvar[:, :, 1], EPS, None, ALU.add))
                    v.sem_inc(s_layer, 1)
                    dve.wait_ge(p_act, n)
                    ch(v.reciprocal(rstd[:, :], rstd[:, :]))
                    for b in range(BLOCKS):
                        done(v.tensor_scalar(nodes[:, b, :], nodes[:, b, :], meanvar[:, b, 0:1], rstd[:, b:b + 1],
                                             ALU.subtract, ALU.mult), "norm")

                if l == 0:
                    pairs(dve, scores_out)
                elif l == 1:
                    pairs(dve, lambda b, u: (epilogue0(b, u), scores_out(b, u)))
                else:
                    pairs(dve, epilogue1)
                    normalise(1, 1)
                    pairs(dve, scores_out)

                def hot(t, l=l):
                    need(dve, "agg", (l * K + t.k - 2) * B)
                    done(v.tensor_tensor(onehot[:, t.u, :, :], iota[:, :].unsqueeze(1).to_broadcast([P, B, P]),
                                         loc[:, bass.ds(t.k * B, B)].unsqueeze(2).to_broadcast([P, B, P]),
                                         ALU.is_equal), "hot")

                def scores(t, l=l, H=H, VV=VV):
                    kk = l * K + t.k
                    n = 2 * H if SELF[l] else H
                    sc = score[:, 0, 0:H * B].rearrange("p (h s) -> p s h", h=H)
                    ad = ps_e[:, AD:AD + n * B].rearrange("p (s n) -> p s n", s=B)
                    need(dve, "scT", kk)
                    need(dve, "ad", kk + 1)
                    dve.wait_ge(s_rows[l][t.u], (t.j + 1) * (16 * B))
                    done(v.tensor_tensor(sc, rows[:, t.u, :, VV:VV + H], ad[:, :, 0:H], ALU.add), "sc1")
                    need(dve, "sc1", kk + 1)
                    if SELF[l]:
                        done(v.tensor_copy(score[:, 1, 0:H * B].rearrange("p (h s) -> p s h", h=H), ad[:, :, H:n]),
                             "sc2")
                    else:
                        need(dve, "dot", (t.k + 1) * B)
                        done(v.tensor_tensor(sc, sc, dots[:, t.u, :, :], ALU.add), "sc2")
                    need(dve, "sc2", kk + 1)
                    s = score[:, 0, 0:H * B]
                    done(v.scalar_tensor_tensor(s, s, SLOPE, s, ALU.mult, ALU.max), "sc")

                def tops(t, l=l, H=H):
                    kk = l * K + t.k
                    R = H * B
                    need(dve, "scp", kk + 1)
                    dve.wait_ge(s_meta[l][t.u], (t.j + 1) * (16 * META[l]))
                    s0 = scoreT[0:R, 0, :]
                    if SELF[l]:
                        done(v.tensor_tensor(top[0:R, 0, :], s0, scoreT[0:R, 1, :], ALU.max), "top0")
                        need(dve, "top0", kk + 1)
                        s0 = top[0:R, 0, :]
                    done(v.tensor_tensor_scan(top[0:R, 1, :], flags[0:R, t.u, PEN_F, :], s0, -BIG,
                                              ALU.add, ALU.max), "topf")

                def tops2(t, l=l, H=H):
                    kk = l * K + t.k
                    R = H * B
                    need(dve, "topf", kk + 1)
                    need(dve, "endp", kk)
                    done(v.tensor_tensor_scan(top[0:R, 2, ::-1], flags[0:R, t.u, PEN_B, ::-1], top[0:R, 1, ::-1],
                                              -BIG, ALU.add, ALU.max), "top")

                def links(t, l=l, H=H):
                    kk = l * K + t.k
                    R = H * (B + 1)
                    e = [ends[0:1, i, 0:R].rearrange("p (h s) -> p h s", h=H) for i in range(2)]
                    r = [ps_row[:, i * 8 * B:i * 8 * B + H * B].rearrange("p (h s) -> p h s", h=H) for i in range(2)]
                    run = runs[0:1, 0, 0:R].rearrange("p (h s) -> p h s", h=H)
                    need(dve, "endp", kk + 1)
                    need(dve, "rdrop", kk)
                    done(v.tensor_copy(e[0][:, :, 1:], r[0]), "ends0")
                    done(v.tensor_copy(e[1][:, :, 0:B], r[1]), "ends1")
                    need(dve, "runl", kk)
                    done(v.tensor_copy(e[0][:, :, 0:1], run[:, :, B:B + 1]), "ends2")

                def links2(t, l=l, H=H):
                    kk = l * K + t.k
                    R = H * (B + 1)
                    need(dve, "ends2", kk + 1)
                    need(dve, "ends0", kk + 1)
                    need(dve, "ends1", kk + 1)
                    need(dve, "link", kk)
                    pen = [chain[0:1, t.u, i, 0:H, :].rearrange("p h s -> p (h s)") for i in range(2)]
                    done(v.tensor_tensor_scan(runs[0:1, 0, 0:R], pen[0], ends[0:1, 0, 0:R], -BIG,
                                              ALU.add, ALU.max), "runl")
                    done(v.tensor_tensor_scan(runs[0:1, 1, 0:R][:, ::-1], pen[1][:, ::-1], ends[0:1, 1, 0:R][:, ::-1],
                                              -BIG, ALU.add, ALU.max), "runr")
                    need(dve, "runr", kk + 1)
                    c = ends[0:1, 0, 0:R].rearrange("p (h s) -> p h s", h=H)[:, :, 0]
                    b = runs[0:1, 1, 0:R].rearrange("p (h s) -> p h s", h=H)[:, :, 0]
                    done(v.tensor_tensor(newtop[0:1, 0:H], c, b, ALU.max), "rnew")
                    need(dve, "rnew", kk + 1)
                    need(dve, "rscale", kk)
                    done(v.tensor_tensor(drop[0:1, 0:H], c, newtop[0:1, 0:H], ALU.subtract), "rdrop")

                def finish_tops(t, l=l, H=H):
                    kk = l * K + t.k
                    R = H * B
                    need(dve, "col", kk + 1)
                    done(v.scalar_tensor_tensor(seg[0:R, :], flags[0:R, t.u, PEN_L, :], ps_col[0:R, 0:1],
                                                top[0:R, 2, :], ALU.add, ALU.max), "seg1")
                    need(dve, "seg1", kk + 1)
                    done(v.scalar_tensor_tensor(seg[0:R, :], flags[0:R, t.u, PEN_R, :], ps_col[0:R, 1:2],
                                                seg[0:R, :], ALU.add, ALU.max), "seg")
                    need(dve, "seg", kk + 1)
                    need(dve, "wp", kk)
                    n = 2 if SELF[l] else 1
                    done(v.tensor_tensor(expT[0:R, 0:n, :], scoreT[0:R, 0:n, :],
                                         seg[0:R, :].unsqueeze(1).to_broadcast([R, n, P]), ALU.subtract), "diff")

                def mask(t, l=l, H=H):
                    kk = l * K + t.k
                    R = H * B
                    need(dve, "exp", kk + 1)
                    done(v.tensor_tensor(expT[0:R, 1, :], expT[0:R, 1, :], flags[0:R, t.u, START, :], ALU.mult),
                         "mask")

                def rescale(t, l=l, H=H, V=V, VV=VV):
                    kk = l * K + t.k
                    need(dve, "fac", kk + 1)
                    need(dve, "w", kk + 1)
                    need(dve, "add", kk * B)
                    b = dve.snap(regs[0], min_val=0, max_val=BLOCKS - 1)
                    s = sums[:, bass.ds(b * VV, VV)].rearrange("p (h c) -> p h c", h=H)
                    done(v.tensor_tensor(s, s, ps_e[:, FAC:FAC + H].unsqueeze(2).to_broadcast([P, H, V]), ALU.mult),
                         "resc")

                def mul(t, s, l=l, H=H, V=V):
                    n = V - 1 if SELF[l] else V
                    r = rows[:, t.u, s, 0:H * V].rearrange("p (h c) -> p h c", h=H)[:, :, 0:n]
                    w = wgt[:, t.u, 0:H * B].rearrange("p (h s) -> p h s", h=H)[:, :, s:s + 1]
                    done(v.tensor_tensor(r, r, w.to_broadcast([P, H, n]), ALU.mult), "mul")

                def add(t, s, l=l, VV=VV):
                    kk = l * K + t.k
                    b = dve.snap(regs[s], min_val=0, max_val=BLOCKS - 1)
                    a = sums[:, bass.ds(b * VV, VV)]
                    need(dve, "agg", kk * B + s + 1)
                    if s:
                        need(dve, "add", kk * B + s)
                    else:
                        need(dve, "resc", kk + 1)
                    done(v.tensor_tensor(a, a, ps_sum[l][s % len(ps_sum[l])][:, 0:VV], ALU.add), "add")

                def dot(t, s):
                    i = t.k * B + s
                    need(dve, "enc", i + 1)
                    need(dve, "dot", i - 1 if s < 2 else i - 2)
                    done(v.tensor_tensor(prod[:, s % 3, :], enc[:, s % 3, :], ps_enc[s % 3][:, D:2 * D], ALU.mult),
                         "prod")

                def dot2(t, s):
                    i = t.k * B + s
                    need(dve, "prod", i + 1)
                    done(v.tensor_reduce(dots[:, t.u, s, :], prod[:, s % 3, :].rearrange("p (h c) -> p h c", h=8),
                                         AX.X, ALU.add), "dot")

                def period(t, left, l=l):
                    n1, n2 = t.after(1), t.after(2)
                    rescale(t)
                    if l != 1:
                        need(dve, "w", l * K + t.k + 1)
                        mul(t, 0)
                    for s in range(B):
                        if l != 1 and s + 1 < B:
                            mul(t, s + 1)
                        enc_here = left > 2 and l == 2 and s >= ENC_AT
                        if enc_here:
                            dot(n2, s - ENC_AT)
                        if left > 2 and s == 0:
                            hot(n2)
                        if left > 1:
                            if s == 1:
                                scores(n1)
                            if s == 2:
                                tops(n1)
                            if s == 3:
                                tops2(n1)
                            if s == 4:
                                links(n1)
                            if s == 5:
                                links2(n1)
                            if s == 6:
                                finish_tops(n1)
                            if s == 7 and SELF[l]:
                                mask(n1)
                        add(t, s)
                        if enc_here:
                            dot2(n2, s - ENC_AT)
                    if left > 2 and l == 2:
                        for s in range(B - ENC_AT, B):
                            dot(n2, s)
                            dot2(n2, s)

                kk = l * K
                run = runs[0:1, 0, 0:H * (B + 1)].rearrange("p (h s) -> p h s", h=H)
                if l:
                    need(dve, "link", kk)
                ch(v.memset(runs[:, :, :], -BIG))
                dve.wait_ge(p_pool, 19 + (1 if l == 1 else 3 if l == 2 else 0))
                if l:
                    need(dve, "rdrop", kk)
                    ch(v.memset(ends[:, :, :], -BIG))
                hot(Batch(0, 0))
                hot(Batch(0, 1))
                if l == 2:
                    for k in range(2):
                        for s in range(B):
                            dot(Batch(0, k), s)
                            dot2(Batch(0, k), s)
                t0 = Batch(0, 0)
                for f in (scores, tops, tops2, links, links2, finish_tops):
                    f(t0)
                if SELF[l]:
                    mask(t0)
                batches(dve, period, lambda t: dve.load(regs, blk[0:1, bass.ds(t.k * BPAD, B)]))

            def epilogue2(b, u):
                W, Hh, Vh = VALS[2], HEADS[2], COLS[2]
                i = 2 * BLOCKS + b
                a = sums[:, bass.ds(b * W, W)].rearrange("p (h c) -> p h c", h=Hh)
                done(v.tensor_scalar(small[:, u, 0, :], a[:, :, Vh - 1], 1e-10, None, ALU.max), "e1")
                need(dve, "e1", i + 1)
                done(v.reciprocal(small[:, u, 1, :], small[:, u, 0, :]), "e4")
                need(dve, "e4", i + 1)
                done(v.tensor_tensor(work2[:, u, :].rearrange("p (h c) -> p h c", h=Hh), a[:, :, 0:CH[2]],
                                     small[:, u, 1, :].unsqueeze(2).to_broadcast([P, Hh, CH[2]]), ALU.mult), "e5")
                need(dve, "e5", i + 1)
                done(v.tensor_tensor(work3[:, u, :], work2[:, u, :], bias[:, 2, :], ALU.add), "e7")
                need(dve, "e7", BLOCKS + b + 1)
                y = nodes[:, bass.ds(b, 1), :].rearrange("p a f -> p (a f)")
                done(v.tensor_tensor(y, y, work3[:, u, :], ALU.add), "e6")
                need_apart(dve, ("e6", i + 1))
                done(v.bn_stats(stats[:, u, :], y), "st2")
                need_apart(dve, ("st2", BLOCKS + b + 1))
                done(v.bn_aggr(mv[:, u, :], stats[:, u, :]), "agr")
                need(dve, "agr", BLOCKS + b + 1)
                done(v.tensor_copy(meanvar[:, bass.ds(b, 1), :].rearrange("p a f -> p (a f)"), mv[:, u, :]), "st1")
            need(dve, "add", 3 * K * B)
            pairs(dve, epilogue2)
            normalise(2, 2)

        @block.sync
        def _(sp):
            s_passed[sp] = sem("s_passed_sp")
            sp.dma_start(nodes[:, 0:FULL, :], x[0:FULL * P, :].rearrange("(b p) f -> p b f", p=P)).then_inc(s_in, 16)
            sp.dma_start(dst_pad[0:E], dst).then_inc(s_pad, 16)
            sp.dma_start(src_pad[0:E], src).then_inc(s_pad, 16)
            sp.dma_start(attr_pad[0:3 * E], edge_attr.rearrange("e j -> (e j)")).then_inc(s_pad, 16)
            sp.wait_ge(p_pool, 5)
            left = TILES * P - E
            sp.dma_start(dst_pad[E:].rearrange("(a n) -> a n", a=1), tail_i[:, 0:left]).then_inc(s_pad, 16)
            sp.dma_start(src_pad[E:].rearrange("(a n) -> a n", a=1), tail_i[:, P:P + left]).then_inc(s_pad, 16)
            sp.dma_start(attr_pad[3 * E:].rearrange("(a n) -> a n", a=1), tail_f[:, 0:3 * left]).then_inc(s_pad, 16)
            sp.dma_start(nodes[0:REST, FULL, :], x[FULL * P:N, :]).then_inc(s_in, 16)
            sp.wait_ge(s_pad, 96)
            sp.dma_start(dst_all, dst_pad.rearrange("(p t) -> p t", p=P)).then_inc(s_dst, 16)
            for w, t in ((w1, wts[0]), (w2, wts[1])):
                sp.dma_start(t[:, :, 0:D], w.rearrange("(c p) n -> p c n", p=P)).then_inc(s_w, 16)
            sp.dma_start(w3in, w3.rearrange("(c p) n -> p c n", p=P)).then_inc(s_w, 16)
            with nc.allow_non_contiguous_dma(reason="768 words, once"):
                sp.dma_start(edgew[0:3, :], edge_w.rearrange("o j -> j o")).then_inc(s_w, 16)
            sp.dma_start(edgew[3:4, :], edge_b.rearrange("(a n) -> a n", a=1)).then_inc(s_w, 16)
            for l, b in enumerate((b1, b2, b3)):
                sp.dma_start(bias[:, l, :], b.partition_broadcast(P)).then_inc(s_w, 16)
            for l, (s, d) in enumerate(((as1, ad1), (as2, ad2), (as3, ad3))):
                if l:
                    sp.wait_ge(p_dve, MARKS[f"AVEC{l - 1}"])
                for i, a in enumerate((s, d)):
                    sp.dma_start(avec[:, i, :], a.rearrange("h c -> (h c)").partition_broadcast(P)).then_inc(s_avec, 16)
            sp.wait_ge(p_dve, MARKS["KEY_DONE"])
            sp.dma_start(keys_d[1:1 + SLOTS * P].rearrange("(c q e) -> q c e", c=4, q=Q), key).then_inc(s_key, 16)
            sp.dma_start(keys_d[0:1].rearrange("(a n) -> a n", a=1), guard[:, 0:1]).then_inc(s_key, 16)
            sp.dma_start(keys_d[SLOTS * P + 1:].rearrange("(a n) -> a n", a=1), guard[:, 1:2]).then_inc(s_key, 16)
            sp.wait_ge(s_key, 48)
            sp.dma_start(kprev, keys_d[0:SLOTS * P].rearrange("(c q e) -> q c e", c=4, q=Q)).then_inc(s_near, 16)
            sp.dma_start(knext, keys_d[2:].rearrange("(c q e) -> q c e", c=4, q=Q)).then_inc(s_near, 16)
            sp.wait_ge(p_dve, MARKS["PREP_DONE"])
            with nc.allow_non_contiguous_dma(reason="short runs, once"):
                sp.dma_start(index_d.rearrange("k p s -> p k s"),
                             index_all.rearrange("p (k s) -> p k s", k=K)).then_inc(s_flag, 16)
                sp.dma_start(chain_d.rearrange("t (c q) -> q t c", c=4),
                             misc[0:Q, 40:48].rearrange("p (t c) -> p t c", t=2)).then_inc(s_flag, 16)
            sp.dma_start(flags_d.rearrange("(c q) f -> q c f", c=4),
                         flg.rearrange("p c t e -> p c (t e)")).then_inc(s_flag, 16)
            for i, v in enumerate((car, car1)):
                sp.dma_start(carry_d[:, i, :].rearrange("(c q) e -> q c e", c=4), v).then_inc(s_flag, 16)
            for j in range(3):
                sp.dma_start(attrT_d[j, :].rearrange("(c q e) -> q c e", c=4, q=Q),
                             attr_t[:, :, j, :]).then_inc(s_flag, 16)
            sp.wait_ge(s_flag, 16 * 8)

            for l in range(3):
                H = HEADS[l]
                def write(b, u, l=l):
                    need_apart(sp, ("tval", l * BLOCKS + b + 1), ("tas", l * BLOCKS + b + 1))
                    sp.dma_start(table[l][bass.ds(b * P, P), :], trow[:, u, 0:ROW[l]]).then_inc(s_tab[l][u], 16)

                if l:
                    need(sp, "add", l * K * B)
                    for u in range(2):
                        sp.wait_ge(s_tab[l - 1][u], 16 * ((BLOCKS + 1 - u) // 2))
                if l == 0:
                    pairs(sp, write)
                elif l == 1:
                    sp.dma_start(self_row[:, 0, 0:VALS[0]], table[0][0:P, 0:VALS[0]]).then_inc(s_self[0][0], 16)
                    sp.dma_start(self_row[:, 1, 0:VALS[0]], table[0][P:2 * P, 0:VALS[0]]).then_inc(s_self[0][1], 16)

                    def refill(b, u):
                        need_apart(sp, ("e2", b + 1))
                        sp.dma_start(self_row[:, u, 0:VALS[0]],
                                     table[0][bass.ds(b * P + 2 * P, P), 0:VALS[0]]).then_inc(s_self[0][u], 16)
                    with sp.Fori(0, (BLOCKS - 3) // 2) as j:
                        for u in range(2):
                            refill(j * 2 + u, u)
                            write(j * 2 + u, u)
                    refill(BLOCKS - 3, 0)
                    for b in range(BLOCKS - 3, BLOCKS):
                        write(b, b % 2)
                else:
                    need(sp, "e2", BLOCKS)
                    sp.dma_start(self_row[:, 0, 0:VALS[1]], table[1][0:P, 0:VALS[1]]).then_inc(s_self[1][0], 16)
                    sp.dma_start(self_row[:, 1, 0:VALS[1]], table[1][P:2 * P, 0:VALS[1]]).then_inc(s_self[1][1], 16)

                    def refill2(b, u):
                        need_apart(sp, ("e2", BLOCKS + b + 1))
                        sp.dma_start(self_row[:, u, 0:VALS[1]],
                                     table[1][bass.ds(b * P + 2 * P, P), 0:VALS[1]]).then_inc(s_self[1][u], 16)
                    with sp.Fori(0, (BLOCKS - 3) // 2) as j:
                        for u in range(2):
                            refill2(j * 2 + u, u)
                    refill2(BLOCKS - 3, 0)
                    pairs(sp, write)

                def meta(t, l=l, H=H):
                    if not isinstance(t.j, int) or t.k >= RING:
                        need_apart(sp, ("resc", l * K + t.k - 2),
                                   ("mask" if SELF[l] else "diff", l * K + t.k - 2),
                                   (s_rows[l][t.u], t.j * (16 * B)))
                    sp.dma_start(index[:, t.u, :], index_d[bass.ds(t.k, 1), :, :].rearrange("a p s -> (a p) s")
                                 ).then_inc(s_index[l][t.u], 16)
                    for h in range(H):
                        sp.dma_start(flags[h * B:(h + 1) * B, t.u, :, :].rearrange("p t e -> p (t e)"),
                                     flags_d[bass.ds(t.k * B, B), :]).then_inc(s_meta[l][t.u], 16)
                    for i, at in ((0, 1), (1, 0)):
                        row = chain_d[i:i + 1, bass.ds(t.k * B, B)]
                        sp.dma_start(chain[0:1, t.u, i, 0:H, at:at + B],
                                     row.unsqueeze(1).to_broadcast([1, H, B])).then_inc(s_meta[l][t.u], 16)
                    sp.dma_start(carry[:, t.u, :], carry_d[bass.ds(t.k * B, 1), :, :].rearrange("a r e -> (a r) e")).then_inc(s_meta[l][t.u], 16)
                    if l == 2:
                        sp.dma_start(attrT[0:3, t.u, :],
                                     attrT_d[:, bass.ds(t.k * B * P, B * P)]).then_inc(s_meta[l][t.u], 16)

                if l == 2:
                    sp.wait_ge(p_pool, 21)
                for k in range(RING):
                    meta(Batch(0, k))
                with sp.Fori(1, K // RING) as j:
                    for u in range(RING):
                        meta(Batch(j, u))
                for k in range(K // RING * RING, K):
                    meta(Batch(k // RING, k % RING))
            for b in range(BLOCKS):
                n = P if b < FULL else REST
                need(sp, "norm", BLOCKS + b + 1)
                sp.dma_start(out[b * P:b * P + n, :], nodes[0:n, b, :]).then_inc(s_out, 16)
            sp.wait_ge(s_out, 16 * BLOCKS)

        @block.gpsimd
        def _(pool):
            s_passed[pool] = sem("s_passed_pool")
            g = nc.gpsimd
            seeded(pool, "e2 e3 tclear")
            g.memset(tail_i[:, 0:P], 100000).then_inc(p_pool, 1)
            g.memset(tail_i[:, P:2 * P], 0).then_inc(p_pool, 1)
            g.memset(tail_f[:, :], 0.0).then_inc(p_pool, 1)
            g.memset(nodes[:, FULL, :], 0.0).then_inc(p_pool, 1)
            g.memset(guard[:, :], -2.0).then_inc(p_pool, 1)
            g.memset(ident[:, :], 0.0).then_inc(p_pool, 1)
            g.iota(iota[:, :], [[1, P]], base=0, channel_multiplier=0,
                   allow_small_or_imprecise_dtypes=True).then_inc(p_pool, 1)
            g.iota(siota, [[B, K], [1, BPAD]], base=0, channel_multiplier=0,
                   allow_small_or_imprecise_dtypes=True).then_inc(p_pool, 1)
            g.iota(siota2, [[1, SLOTS]], base=0, channel_multiplier=0,
                   allow_small_or_imprecise_dtypes=True).then_inc(p_pool, 1)
            g.iota(misc[:, 0:1], [[0, 1]], base=0, channel_multiplier=1,
                   allow_small_or_imprecise_dtypes=True).then_inc(p_pool, 1)
            g.iota(misc[:, 4:8], [[Q, 4]], base=0, channel_multiplier=1,
                   allow_small_or_imprecise_dtypes=True).then_inc(p_pool, 1)
            g.memset(ones[:, :], 1.0).then_inc(p_pool, 1)
            g.memset(zeros[:, :], 0.0).then_inc(p_pool, 1)
            pool.wait_ge(p_pool, 6)
            g.affine_select(out=ident[:, :], in_=ident[:, :], compare_op=ALU.not_equal, fill=1.0, base=0,
                            pattern=[[-1, P]], channel_multiplier=1).then_inc(p_pool, 1)
            g.memset(carry[:, :, :], 1.0).then_inc(p_pool, 1)
            g.memset(scale[:, :], 1.0).then_inc(p_pool, 1)
            g.memset(chain[:, :, :, :, :], -BIG).then_inc(p_pool, 1)
            g.memset(ends[:, :, :], -BIG).then_inc(p_pool, 1)
            pool.wait_ge(p_dve, MARKS["TILE_DONE"])
            tcol = misc[:, 16:20].bitcast(I32)
            for c in range(4):
                for to, frm in ((dst_g[:, c * P:(c + 1) * P], dst_pad.rearrange("(t e) -> t e", e=P)),
                                (src_g[:, c * P:(c + 1) * P], src_pad.rearrange("(t e) -> t e", e=P)),
                                (attr_g[:, c, :, :].rearrange("p e j -> p (e j)"),
                                 attr_pad.rearrange("(t e) -> t e", e=3 * P))):
                    g.indirect_dma_start(out=to, out_offset=None, in_=frm,
                                         in_offset=bass.IndirectOffsetOnAxis(ap=tcol[0:Q, c:c + 1], axis=0)
                                         ).then_inc(s_got, 16)
            pool.wait_ge(s_flag, 16 * 8)
            g.memset(sums[:, :], 0.0).then_inc(p_pool, 1)

            for l in range(3):
                base = l * BLOCKS
                if l == 2:
                    pool.wait_ge(s_flag, 16 * 8)
                    g.memset(attrT[:, :, :], 1.0).then_inc(p_pool, 1)
                if l == 1:
                    def selfs(b, u):
                        H, C, V = HEADS[0], COLS[0], VALS[0]
                        q = small[:, u, 0, 0:H]
                        need(pool, "e1", b + 1)
                        pool.wait_ge(s_self[0][u], (b - u) * 8 + 16)
                        need(pool, "e5", b - 1)
                        t = work[:, u, 0:V].rearrange("p (h c) -> p h c", h=H)[:, :, 0:C - 1]
                        r = self_row[:, u, 0:V].rearrange("p (h c) -> p h c", h=H)[:, :, 0:C - 1]
                        a = sums[:, bass.ds(b * V, V)].rearrange("p (h c) -> p h c", h=H)[:, :, 0:C - 1]
                        done(g.tensor_tensor(t, r, q.unsqueeze(2).to_broadcast([P, H, C - 1]), ALU.mult), "e2")
                        need(pool, "e2", b + 1)
                        done(g.tensor_tensor(t, t, a, ALU.add), "e3")
                    with pool.Fori(0, BLOCKS // 2) as j:
                        selfs(j * 2, 0)
                        selfs(j * 2 + 1, 1)
                    selfs(BLOCKS - 1, 0)
                if l:
                    need(pool, "e3" if l == 1 else "e2", BLOCKS if l == 1 else 2 * BLOCKS)
                    g.memset(sums[:, :], 0.0).then_inc(p_pool, 1)
                need(pool, "tself" if SELF[l] else "tad", base + BLOCKS)
                for u in range(2):
                    pool.wait_ge(s_tab[l][u], 16 * ((BLOCKS + 1 - u) // 2))

                def gather(t, l=l):
                    if not isinstance(t.j, int) or t.k >= RING:
                        need_apart(pool, ("agg", (t.k + (l * K - 2)) * B), (s_index[l][t.u], t.j * 16 + 16))
                    else:
                        pool.wait_ge(s_index[l][t.u], t.j * 16 + 16)
                    for s in range(B):
                        g.indirect_dma_start(out=rows[:, t.u, s, 0:ROW[l]], out_offset=None, in_=table[l],
                                             in_offset=bass.IndirectOffsetOnAxis(ap=index[:, t.u, s:s + 1], axis=0)
                                             ).then_inc(s_rows[l][t.u], 16)
                for k in range(RING):
                    gather(Batch(0, k))
                with pool.Fori(1, K // RING) as j:
                    for u in range(RING):
                        gather(Batch(j, u))
                for k in range(K // RING * RING, K):
                    gather(Batch(k // RING, k % RING))

        @block.scalar
        def _(act):
            s_passed[act] = sem("s_passed_act")
            a = nc.scalar
            seeded(act, "link hotT scp rscale exp w enc ycopy yT tval ex")
            for l in range(3):
                H, C, V = HEADS[l], CH[l], COLS[l]
                base = l * BLOCKS

                def node(b, u, l=l, H=H, C=C, V=V, base=base):
                    if l != 1:
                        need(act, "yTp", base + b - 1)
                        need(act, "norm", 0 if l == 0 else b + 1)
                        if l == 0:
                            act.wait_ge(s_in, 32)
                        done(a.copy(yin[:, u, :], nodes[:, bass.ds(b, 1), :].rearrange("p a f -> p (a f)")), "ycopy")
                    else:
                        need(act, "e7", b + 1)
                        need(act, "e8", b - 1)
                        done(a.activation(expo[:, u, :], work3[:, u, :], ACT.Exp), "ex")
                    need(act, "yp", base + b - 1)
                    need(act, "yTp", base + b + 1)
                    done(a.copy(yT[:, u, :, :].rearrange("p c n -> p (c n)"), ps_yT[u][:, 0:2 * P]), "yT")
                    need(act, "yp", base + b + 1)
                    free(act, s_tab[l][u], b, u)
                    if l == 2:
                        a.copy(hnode[:, bass.ds(b, 1), :].rearrange("p a f -> p (a f)"), ps_y[u][:, 0:D])
                    done(a.copy(trow[:, u, 0:H * V].rearrange("p (h c) -> p h c", h=H)[:, :, 0:C],
                                ps_y[u][:, 0:D].rearrange("p (h c) -> p h c", h=H)), "tval")

                act.wait_ge(p_pool, 13)
                if l == 2:
                    act.wait_ge(s_flag, 16 * 8)
                if l == 0:
                    act.wait_ge(p_dve, MARKS["ONES_DONE"])
                if l == 2:
                    act.wait_ge(s_layer, 1)
                    a.activation(rstd[:, :], meanvar[:, :, 1], ACT.Sqrt).then_inc(p_act, 1)
                pairs(act, node)

                def hotT(t, g, l=l):
                    kk = l * K + t.k
                    need(act, "hotp", 3 * kk + g + 1)
                    if g == 0:
                        need(act, "ad", kk - 2)
                        if l == 2:
                            need(act, "encp", (t.k - 2) * B)
                    n = min(4, B - 4 * g)
                    done(a.copy(onehotT[:, t.u, 4 * g:4 * g + n, :].rearrange("p s e -> p (s e)"),
                                ps_hot[:, 0:n * P]), "hotT")

                def scores(t, l=l, H=H):
                    kk = l * K + t.k
                    n = 2 if SELF[l] else 1
                    need(act, "scT", kk + 1)
                    done(a.copy(scoreT[0:H * B, 0:n, :].rearrange("p a e -> p (a e)"),
                                ps_T[0:H * B, 0:n * P]), "scp")

                def link(t, l=l, H=H):
                    kk = l * K + t.k
                    need(act, "runr", kk + 1)
                    need(act, "col", kk)
                    for i in range(2):
                        r = a.copy(linkrow[0:1, i, 0:H * B].rearrange("p (h s) -> p h s", h=H),
                                   runs[0:1, i, 0:H * (B + 1)].rearrange("p (h s) -> p h s", h=H)[:, :, i:i + B])
                    done(r, "link")

                def rescale(t, l=l, H=H):
                    kk = l * K + t.k
                    need(act, "rdrop", kk + 1)
                    need(act, "fac", kk)
                    done(a.activation(scale[0:1, 0:H], drop[0:1, 0:H], ACT.Exp), "rscale")

                def expw(t, l=l, H=H):
                    kk = l * K + t.k
                    n = 2 if SELF[l] else 1
                    need(act, "diff", kk + 1)
                    done(a.activation(expT[0:H * B, 0:n, :], expT[0:H * B, 0:n, :], ACT.Exp), "exp")

                def weights(t, l=l, H=H, V=V):
                    kk = l * K + t.k
                    need(act, "wp", kk + 1)
                    if SELF[l]:
                        a.copy(rows[:, t.u, :, 0:H * V].rearrange("p s (h c) -> p h s c", h=H)[:, :, :, V - 1],
                               ps_e[:, QT:QT + H * B].rearrange("p (h s) -> p h s", h=H))
                    done(a.copy(wgt[:, t.u, 0:H * B], ps_e[:, WT:WT + H * B]), "w")

                def encode(t, s):
                    i = t.k * B + s
                    need(act, "encp", i + 1)
                    need(act, "prod", i - 1 if s < 2 else i - 2)
                    done(a.activation(enc[:, s % 3, :], ps_enc[s % 3][:, 0:D], ACT.Relu), "enc")

                def mul_act(t, s, l=l, V=V):
                    done(a.activation(rows[:, t.u, s, 0:V - 1], rows[:, t.u, s, 0:V - 1], ACT.Copy,
                                      scale=wgt[:, t.u, s:s + 1]), "mul")

                def period(t, left, l=l):
                    n1, n2 = t.after(1), t.after(2)
                    if l == 1:
                        need(act, "w", l * K + t.k + 1)
                        mul_act(t, 0)
                    for s in range(B):
                        if l == 1 and s + 1 < B:
                            mul_act(t, s + 1)
                        if left > 2 and s in (1, 2, 3):
                            hotT(n2, s - 1)
                        if left > 2 and l == 2 and s >= ENC_AT:
                            encode(n2, s - ENC_AT)
                        if left > 1:
                            if s == 2:
                                scores(n1)
                            if s == 5:
                                link(n1)
                            if s == 6:
                                rescale(n1)
                            if s == 7:
                                expw(n1)
                            if s == 8:
                                weights(n1)
                    if left > 2 and l == 2:
                        for s in range(B - ENC_AT, B):
                            encode(n2, s)

                for t in (Batch(0, 0), Batch(0, 1)):
                    for gg in range(3):
                        hotT(t, gg)
                    if l == 2:
                        for s in range(B):
                            encode(t, s)
                for f in (scores, link, rescale, expw, weights):
                    f(Batch(0, 0))
                batches(act, period, lambda t: None)
            act.wait_ge(s_layer, 2)
            a.activation(rstd[:, :], meanvar[:, :, 1], ACT.Sqrt).then_inc(p_act, 1)

        @block.tensor
        def _(pe):
            s_passed[pe] = sem("s_passed_pe")
            m = nc.tensor
            seeded(pe, "hotp ad scT endp fac col wp agg encp yTp yp")
            regs = block_regs(pe, "blk_pe")
            regs2 = block_regs(pe, "blk_pe2")
            pe.wait_ge(p_pool, 18)
            pe.wait_ge(p_dve, MARKS["COUNT_DONE"])
            m.matmul(ps_e[0:BLOCKS - 1, 0:1], counts, ones[:, :], start=True, stop=True).then_inc(p_pe, 1)
            pe.wait_ge(p_dve, MARKS["GT_DONE"])
            m.matmul(ps_T[0:1, 0:K * BPAD], ones[0:BLOCKS - 1, :], slot_gt, start=True, stop=True).then_inc(p_pe, 1)
            for c in range(4):
                m.matmul(ps_hot[0:Q, c:c + 1], slot_gt2[:, c * Q:(c + 1) * Q], ones[0:BLOCKS - 1, :],
                         start=True, stop=True).then_inc(p_pe, 1)
            pe.wait_ge(p_dve, MARKS["LOC_DONE"])
            for i, v in enumerate((loc_g, srcf)):
                for c in range(4):
                    m.transpose(bank[3 + i][:, c * Q:(c + 1) * Q], v[:, c, :], ident[0:Q, 0:Q]).then_inc(p_pe, 1)
            pe.wait_ge(s_w, 16 * 8)
            for c in range(2):
                for o in range(2):
                    m.transpose(bank[5][:, c * D + o * P:c * D + (o + 1) * P], w3in[:, o, c * P:(c + 1) * P],
                                ident[:, :]).then_inc(p_pe, 1)

            for l in range(3):
                H, C, V, VV = HEADS[l], CH[l], COLS[l], VALS[l]
                base = l * BLOCKS

                def node(b, u, l=l, H=H, base=base):
                    need(pe, "ycopy" if l == 0 else ("e8" if l == 1 else "ycopy"),
                         b + 1 if l < 2 else BLOCKS + b + 1)
                    need(pe, "yT", base + b - 1)
                    for c in range(2):
                        i = m.transpose(ps_yT[u][:, c * P:(c + 1) * P], yin[:, u, c * P:(c + 1) * P], ident[:, :])
                    done(i, "yTp")
                    need(pe, "yT", base + b + 1)
                    need(pe, "tval", base + b - 1)
                    need(pe, "tad", base + b - 1)
                    for c in range(2):
                        i = m.matmul(ps_y[u][:, 0:D + 2 * H], yT[:, u, c, :], wts[l][:, c, :],
                                     start=(c == 0), stop=(c == 1))
                    done(i, "yp")

                pe.wait_ge(p_dve, MARKS["WA_DONE"])
                pairs(pe, node)

                def hot(t, g, l=l):
                    kk = l * K + t.k
                    if g == 0:
                        need(pe, "hot", kk + 1)
                    need(pe, "hotT", 3 * kk + g)
                    for i in range(min(4, B - 4 * g)):
                        r = m.transpose(ps_hot[:, i * P:(i + 1) * P], onehot[:, t.u, 4 * g + i, :], ident[:, :])
                    done(r, "hotp")

                def adst(t, l=l, H=H):
                    kk = l * K + t.k
                    n = 2 * H if SELF[l] else H
                    load(t, regs)
                    need(pe, "hotT", 3 * kk + 3)
                    need(pe, "resc", kk)
                    for s in range(B):
                        b = pe.snap(regs[s], min_val=0, max_val=BLOCKS - 1)
                        r = m.matmul(ps_e[:, AD + s * n:AD + (s + 1) * n], onehotT[:, t.u, s, :],
                                     dtab[:, bass.ds(b, 1), 0:n].rearrange("p a n -> p (a n)"),
                                     start=True, stop=True)
                    done(r, "ad")

                def scoresT(t, l=l, H=H):
                    kk = l * K + t.k
                    need_apart(pe, ("sc", kk + 1), ("diff", kk))
                    for i in range(2 if SELF[l] else 1):
                        r = m.transpose(ps_T[0:H * B, i * P:(i + 1) * P], score[:, i, 0:H * B], ident[:, :])
                    done(r, "scT")

                def endsT(t, l=l, H=H):
                    kk = l * K + t.k
                    need_apart(pe, ("top", kk + 1))
                    for i, e in enumerate((P - 1, 0)):
                        r = m.transpose(ps_row[:, i * 8 * B:i * 8 * B + H * B], top[0:H * B, 2, e:e + 1],
                                        ident[0:H * B, 0:H * B])
                    done(r, "endp")

                def cols(t, l=l, H=H):
                    kk = l * K + t.k
                    need_apart(pe, ("link", kk + 1))
                    for i in range(2):
                        r = m.matmul(ps_col[0:H * B, i:i + 1], linkrow[0:1, i, 0:H * B], ones[0:1, :], start=True, stop=True)
                    done(r, "col")

                def factor(t, l=l, H=H):
                    kk = l * K + t.k
                    need(pe, "rscale", kk + 1)
                    need(pe, "resc", kk)
                    m.matmul(ps_e[:, FAC:FAC + H], carry[:, t.u, :], scale[:, 0:H],
                             start=True, stop=True).then_inc(ev["fac"], 1)

                def weightsT(t, l=l, H=H):
                    kk = l * K + t.k
                    need_apart(pe, ("exp", kk + 1), ("w", kk))
                    m_ = m.transpose(ps_e[:, WT:WT + H * B], expT[0:H * B, 0, :], ident[0:H * B, 0:H * B])
                    if SELF[l]:
                        need_apart(pe, ("mask", kk + 1))
                        m_ = m.transpose(ps_e[:, QT:QT + H * B], expT[0:H * B, 1, :], ident[0:H * B, 0:H * B])
                    done(m_, "wp")

                def sum_slot(t, s, l=l, VV=VV):
                    i = (l * K + t.k) * B + s
                    nb = len(ps_sum[l])
                    need(pe, "mul", i + 1)
                    need(pe, "add", (l * K + t.k) * B + (s - nb + 1 if s >= nb else 0))
                    done(m.matmul(ps_sum[l][s % nb][:, 0:VV], onehot[:, t.u, s, :], rows[:, t.u, s, 0:VV],
                                  start=True, stop=True), "agg")

                def encode(t, s):
                    i = t.k * B + s
                    need(pe, "prod", i - 1 if s < 2 else i - 2)
                    if s == 0:
                        pe.wait_ge(s_meta[2][t.u], (t.j + 1) * 16 * META[2])
                    if s % 4 == 0:
                        need(pe, "hotT", 3 * (2 * K + t.k) + s // 4 + 1)
                    p = ps_enc[s % 3]
                    m.matmul(p[:, 0:D], attrT[:, t.u, s * P:(s + 1) * P], edgew[:, :], start=True, stop=True)
                    b = pe.snap(regs2[s], min_val=0, max_val=BLOCKS - 1)
                    done(m.matmul(p[:, D:2 * D], onehotT[:, t.u, s, :],
                                  hnode[:, bass.ds(b, 1), :].rearrange("p a f -> p (a f)"),
                                  start=True, stop=True), "encp")

                def load(t, rr):
                    pe.load(rr, blk[0:1, bass.ds(t.k * BPAD, B)])

                def period(t, left, l=l):
                    n1, n2 = t.after(1), t.after(2)
                    if left > 2 and l == 2:
                        load(n2, regs2)
                    for s in range(B):
                        sum_slot(t, s)
                        if left > 2 and s in (1, 2, 3):
                            hot(n2, s - 1)
                        if left > 2 and l == 2 and s >= ENC_AT:
                            encode(n2, s - ENC_AT)
                        if left > 1:
                            if s == 0:
                                adst(n1)
                            if s == 2:
                                scoresT(n1)
                            if s == 4:
                                endsT(n1)
                            if s == 6:
                                cols(n1)
                            if s == 7:
                                factor(n1)
                            if s == 8:
                                weightsT(n1)
                    if left > 2 and l == 2:
                        for s in range(B - ENC_AT, B):
                            encode(n2, s)

                need(pe, "tself" if SELF[l] else "tad", base + BLOCKS)
                if l == 2:
                    need(pe, "tval", base + BLOCKS)
                for t in (Batch(0, 0), Batch(0, 1)):
                    if l == 2:
                        load(t, regs2)
                    for gg in range(3):
                        hot(t, gg)
                    if l == 2:
                        for s in range(B):
                            encode(t, s)
                for f in (adst, scoresT, endsT, cols, factor, weightsT):
                    f(Batch(0, 0))
                batches(pe, period, lambda t: None)


_INS = ("x", "src", "dst", "edge_attr_3", "L0_gnn_W1", "L0_gnn_a_src1", "L0_gnn_a_dst1", "L0_gnn_b1", "L0_gnn_W2",
        "L0_gnn_a_src2", "L0_gnn_a_dst2", "L0_gnn_b2", "L1_gnn_W", "L1_gnn_a_src", "L1_gnn_a_dst", "L1_gnn_edge_W",
        "L1_gnn_edge_b", "L1_gnn_bias")


def kernel(**inputs):
    import numpy as np
    import concourse.bacc as bacc
    from concourse.bass_utils import run_bass_kernel_spmd

    nc = bacc.Bacc("TRN2", target_bir_lowering=False, num_devices=1)
    arrays, args = {}, []
    for name in _INS:
        a = np.ascontiguousarray(inputs[name])
        arrays[f"in_{name}"] = a
        args.append(nc.dram_tensor(f"in_{name}", a.shape, mybir.dt.from_np(a.dtype), kind="ExternalInput").ap())
    out = nc.dram_tensor("out", (N, D), F32, kind="ExternalOutput").ap()
    gat_kernel(nc, *args, out)
    r = run_bass_kernel_spmd(nc, [arrays], core_ids=[0])
    return r.results[0]["out"]
```

```python
from contextlib import ExitStack

import concourse.bass as bass
from concourse import mybir

F32 = mybir.dt.float32
I32 = mybir.dt.int32
BF16 = mybir.dt.bfloat16
ALU = mybir.AluOpType
ACT = mybir.ActivationFunctionType
AX = mybir.AxisListType

P = 128
N = 3125
D = 256
E = 53125
BLOCKS = -(-N // P)
FULL = N // P
REST = N - FULL * P
TILES = -(-E // P)
SLOTS = TILES + BLOCKS - 1
B = 11
K = SLOTS // B
BPAD = 12
Q = SLOTS // 4
BIG = 1.0e30
RING = 3
EPS = 1e-5
SLOPE = 0.2
SEED = 4
GATHERS = ((0, 4), (4, 8), (8, B))
assert SLOTS == B * K and SLOTS == 4 * Q and Q <= P

HEADS = (4, 1, 8)
CH = tuple(D // h for h in HEADS)
COLS = (CH[0] + 2, CH[1] + 2, CH[2] + 1)
VALS = tuple(h * c for h, c in zip(HEADS, COLS))
ROW = tuple(v + h for v, h in zip(VALS, HEADS))
VMAX, RMAX = max(VALS), max(ROW)
SELF = (True, True, False)
META = tuple(h + 4 + 3 * (not s) for h, s in zip(HEADS, SELF))
HOTS = ((0, 6), (6, B))
OWNER = ("VAVVAVAVVVV", "VAAAAAAAAAA", "AVPVVPAVPVP")
OWN = tuple({e: tuple(s for s in range(B) if o[s] == e) for e in "VAP"} for o in OWNER)
LEAD = (2, 2, 2)

PEN_F, PEN_B, PEN_L, PEN_R, START = range(5)

AT = (
    dict(tops2=1, links=3, finish=5, mask=6, scores=7, tops=10, hot=4, load=5, encV=0,
         link=5, exp=7, weights=8, hotT=3, copy=8, encA=0,
         endsT=2, cols=4, weightsT=7, hotP=1, adst=6, scoresT=9, encP=0),
    dict(tops2=0, links=1, finish=5, mask=6, scores=7, tops=10, hot=3, load=8, encV=0,
         link=2, exp=7, weights=7, hotT=0, copy=7, encA=0,
         endsT=1, cols=4, weightsT=7, hotP=0, adst=5, scoresT=8, encP=0),
    dict(tops2=0, links=1, finish=4, mask=10, scores=8, tops=10, hot=0, load=7, encV=1,
         link=3, exp=5, weights=7, hotT=1, copy=9, encA=1,
         endsT=1, cols=4, weightsT=5, hotP=1, adst=1, scoresT=9, encP=1),
)


class Batch:

    def __init__(self, j, u):
        self.j, self.u = (j + u // RING), u % RING
        self.k = self.j * RING + self.u

    def after(self, n):
        return Batch(self.j, self.u + n)


def gat_kernel(nc, x, src, dst, edge_attr, w1, as1, ad1, b1, w2, as2, ad2, b2, w3, as3, ad3, edge_w, edge_b, b3, out):
    ctx = ExitStack()
    with ctx:
        def sb(name, shape, dt=F32):
            return ctx.enter_context(nc.sbuf_tensor(name, shape, dt))

        def dram(name, shape, dt=F32):
            return nc.dram_tensor(name, shape, dt, kind="Internal").ap()

        def sem(name):
            return ctx.enter_context(nc.semaphore(name))

        dst_pad = dram("dst_pad", (TILES * P,), I32)
        src_pad = dram("src_pad", (TILES * P,), I32)
        attr_pad = dram("attr_pad", (TILES * P * 3,))
        keys_d = dram("keys_d", (SLOTS * P + 2,))
        flags_d = dram("flags_d", (SLOTS, 5 * P))
        chain_d = dram("chain_d", (2, SLOTS))
        carry_d = dram("carry_d", (SLOTS, 2, P))
        index_d = dram("index_d", (K, P, B), I32)
        attrT_d = dram("attrT_d", (9, SLOTS * P), BF16)
        loc_d = dram("loc_d", (SLOTS * P,), BF16)
        table = [dram(f"table{l}", (BLOCKS * P, ROW[l])) for l in range(3)]

        nodes = sb("nodes", [P, BLOCKS, D])
        sums = sb("sums", [P, BLOCKS * VMAX])
        late = sb("late", [P, (BLOCKS * 3 * D + RING * B * P) // 2])
        rows = sb("rows", [P, RING, B, RMAX])
        onehot = sb("onehot", [P, RING, B, P])
        onehotT = sb("onehotT", [P, RING, B * P], BF16)
        locb = sb("locb", [P, RING, B * P], BF16)
        flags = sb("flags", [8 * B, RING, 5, P])
        chain = sb("chain", [1, RING, 2, 8, B + 1])
        carry = sb("carry", [2, RING, P])
        index = sb("index", [P, RING, B], I32)
        blk = sb("blk", [1, K * BPAD], I32)
        ntab = sb("ntab", [P, BLOCKS, 16])
        dtab = sb("dtab", [P, BLOCKS, 8])
        dtab3 = sb("dtab3", [P, BLOCKS, 3, 8], BF16)
        score = sb("score", [P, 2, 8 * B])
        adsum = sb("adsum", [P, 8 * B])
        scoreT = sb("scoreT", [8 * B, 2, P])
        top = sb("top", [8 * B, 3, P])
        seg = sb("seg", [8 * B, P])
        expT = sb("expT", [8 * B, 2, P])
        ends = sb("ends", [1, 2, 8 * (B + 1)])
        runs = sb("runs", [1, 2, 8 * (B + 1)])
        linkrow = sb("linkrow", [1, 2, 8 * B])
        newtop = sb("newtop", [1, 8])
        drop = sb("drop", [1, 8])
        scale = sb("scale", [2, 8])
        wgt = sb("wgt", [P, RING, 8 * B])
        prod = sb("prod", [P, 3, D])
        dots = sb("dots", [P, RING, B, 8])
        wts = [sb(f"wts{l}", [P, 2, D + 2 * HEADS[l]]) for l in range(3)]
        bias = sb("bias", [P, 3, D])
        edgew3 = sb("edgew3", [30, D], BF16)
        ident = sb("ident", [P, P])
        identb = sb("identb", [P, P], BF16)
        pidx = sb("pidx", [P, 1])
        ones = sb("ones", [P, 1])
        flat = rows[:, :, :, :].rearrange("p r s c -> p (r s c)")
        at = [0]

        def tile(*shape):
            n = 1
            for d in shape:
                n *= d
            at[0] += n
            t = flat[:, at[0] - n:at[0]]
            if len(shape) == 1:
                return t
            return t.rearrange("p (u c) -> p u c", u=shape[0]) if len(shape) == 2 else t.rearrange(
                "p (u c n) -> p u c n", u=shape[0], c=shape[1])
        yin, yT, trow = tile(2, D), tile(2, 2, P), tile(2, RMAX)
        self_row, work = tile(2, VMAX), tile(2, VMAX)
        work2, work3, expo = tile(2, D), tile(2, D), tile(2, D)
        avec = tile(6, D)
        edgewr = work3[0:4, 0, :]
        edgew = prod[0:4, 0, :]
        edgew_p = prod[0:4, 1:3, :].rearrange("p i f -> p (i f)")[:, 0:3 * D // 2].bitcast(BF16).rearrange(
            "p (i f) -> p i f", i=3)
        small = sb("small", [P, 2, 4, 8])
        stats = sb("stats", [P, 2, 6])
        mv = sb("mv", [P, 2, 2])
        meanvar = sb("meanvar", [P, BLOCKS, 2])
        rstd = sb("rstd", [P, BLOCKS])

        lateb = late[:, :].bitcast(BF16)
        hnode3 = lateb[:, 0:BLOCKS * 3 * D].rearrange("p (b i f) -> p b i f", b=BLOCKS, i=3)
        attrT = lateb[0:30, BLOCKS * 3 * D:].rearrange("p (r f) -> p r f", r=RING)

        def part(at, n, p=Q):
            return late[0:p, at:at + n]
        flg = part(0, 4 * 5 * P).rearrange("p (c t e) -> p c t e", c=4, t=5)
        attr_g = part(2560, 1536).rearrange("p (c e j) -> p c e j", c=4, j=3)
        attr_p = part(4096, 1536 * 3 // 2).bitcast(BF16).rearrange("p (i c j e) -> p i c j e", i=3, c=4, j=3)
        loc_b = part(6400, 256).bitcast(BF16)
        car = part(10752, 512).rearrange("p (c e) -> p c e", c=4)
        iota = part(11264, P, P)
        dst_g = part(6656, 512).bitcast(I32)
        src_g = part(10240, 512).bitcast(I32)
        dstf, srcf, loc_g, key, kprev, knext = (
            part(7168 + 512 * i, 512).rearrange("p (c e) -> p c e", c=4) for i in range(6))
        dst_all = sums[:, 0:TILES].bitcast(I32)
        dst_allf = sums[:, TILES:2 * TILES]
        dead = sums[:, 2 * TILES:3 * TILES]
        slot_gt = sums[0:BLOCKS - 1, 1248:1248 + K * BPAD]
        slot_gt2 = sums[0:BLOCKS - 1, 1728:1728 + SLOTS]
        siota = sums[0:BLOCKS - 1, 2168:2168 + K * BPAD]
        siota2 = sums[0:BLOCKS - 1, 2648:2648 + SLOTS]
        counts = sums[:, 3088:3088 + BLOCKS - 1]
        misc = sums[:, 3120:3200]
        guard = sums[0:1, 3200:3202]
        tail_i = sums[0:1, 3300:3300 + 2 * P].bitcast(I32)
        tail_f = sums[0:1, 3600:3600 + 3 * P]
        index_all = sums[:, 5200:5200 + SLOTS].bitcast(I32)
        car1 = sums[0:Q, 5700:6212].rearrange("p (c e) -> p c e", c=4)
        attr_r = sums[0:Q, 0:1536].rearrange("p (c e j) -> p c e j", c=4, j=3)
        w3in = sums[:, 4000:4000 + 2 * D].rearrange("p (c n) -> p c n", c=2)
        wprod = sums[:, 4600:4600 + 2 * D].rearrange("p (c n) -> p c n", c=2)

        bank = [ctx.enter_context(nc.psum_tensor(f"bank{i}", [P, 512], F32)) for i in range(8)]
        ps_hot, ps_T, ps_e = bank[0], bank[1], bank[2]
        ps_hotb = [[bank[i][:, :].bitcast(BF16) for i in two] for two in ((0, 7), (0, 7), (0, 0))]
        AD, WT, QT, FAC = 0, 264, 352, 440
        ps_row = ps_T[0:1, 256:256 + 2 * 8 * B]
        ps_col = ps_T[0:8 * B, 440:442]
        ps_sum = ([bank[i] for i in (3, 4, 5, 6)], [bank[i] for i in (3, 4, 5, 6)], [bank[i] for i in (3, 4)])
        ps_enc = [bank[i] for i in (5, 6, 7)]
        ps_yT = [bank[i] for i in (3, 4)]
        ps_y = [bank[i] for i in (5, 6)]

        names = (
            "hot hotp hotT "
            "ad sc1 sc2 sc3 sc "
            "scT scp top0 topf top "
            "endp ends0 ends1 ends2 runl runr "
            "link col seg1 seg "
            "rnew rdrop rscale fac resc "
            "diff exp mask wp w "
            "mulv mula mulp agg add "
            "encp enc prod dot "
            "ycopy yTp yT yp tval tad "
            "h1 h2 h3 "
            "e1 e2 e3 e4 e5 e6 e7 ex branch e8 "
            "self2 sum stat aggr kept norm").split()
        ev = {n: sem("ev_" + n) for n in names}
        s_passed = {}
        s_in = sem("s_in")
        s_pad = sem("s_pad")
        s_w = sem("s_w")
        s_avec = [sem(f"s_avec{l}") for l in range(3)]
        s_dst = sem("s_dst")
        s_got = sem("s_got")
        s_key = sem("s_key")
        s_near = sem("s_near")
        s_flag = sem("s_flag")
        p_pool, p_dve, p_pe, p_act = sem("p_pool"), sem("p_dve"), sem("p_pe"), sem("p_act")
        s_dpad = sem("s_dpad")
        s_w0 = sem("s_w0")
        s_parts = sem("s_parts")
        s_bias = sem("s_bias")
        s_layer = sem("s_layer")
        s_index = [[sem(f"s_index{l}_{u}") for u in range(RING)] for l in range(3)]
        s_meta = [[sem(f"s_meta{l}_{u}") for u in range(RING)] for l in range(3)]
        s_rows = [[sem(f"s_rows{l}_{u}") for u in range(RING)] for l in range(3)]
        s_tab = [[sem(f"s_tab{l}_{u}") for u in range(2)] for l in range(3)]
        s_self = [[sem(f"s_self{l}_{u}") for u in range(2)] for l in range(2)]
        s_out = sem("s_out")

        def need(eng, name, count):
            if isinstance(count, int) and count <= 0:
                return
            eng.wait_ge(ev[name], count + SEED)

        def need_apart(eng, *waits):
            for w, c in waits:
                if isinstance(w, str):
                    need(eng, w, c)
                else:
                    eng.wait_ge(w, c)
                if not isinstance(c, int):
                    eng.sem_inc(s_passed[eng], 1)

        def seeded(eng, which):
            for n in which.split():
                eng.sem_inc(ev[n], SEED)

        def done(inst, name):
            return inst.then_inc(ev[name], 1)

        def free(eng, s, b, u):
            if not isinstance(b, int) or b > 1:
                eng.wait_ge(s, (b - u) * 8)

        def pairs(eng, body):
            body(0, 0)
            body(1, 1)
            with eng.Fori(1, BLOCKS // 2) as j:
                body(j * 2, 0)
                body(j * 2 + 1, 1)
            body(BLOCKS - 1, 0)

        def twos(eng, *steps):
            def group(blocks):
                for step in steps:
                    for b, u in blocks:
                        step(b, u)
            group([(0, 0), (1, 1)])
            with eng.Fori(1, BLOCKS // 2) as j:
                group([(j * 2, 0), (j * 2 + 1, 1)])
            group([(BLOCKS - 1, 0)])

        def staggered(eng, *steps):
            most = max(ahead for _, ahead in steps)

            def at_block(i):
                for body, ahead in steps:
                    if 0 <= i + ahead < BLOCKS:
                        body(i + ahead, (i + ahead) % 2)
            for i in range(-most, 2):
                at_block(i)
            end = (BLOCKS - most) // 2
            with eng.Fori(1, end) as j:
                for u in range(2):
                    for body, ahead in steps:
                        body(j * 2 + (u + ahead), (u + ahead) % 2)
            for i in range(2 * end, BLOCKS):
                at_block(i)

        def weighted(eng, l, k, s):
            e = OWNER[l][s]
            before = sum(K * len(OWN[i][e]) for i in range(l))
            need(eng, {"V": "mulv", "A": "mula", "P": "mulp"}[e],
                 before + k * len(OWN[l][e]) + OWN[l][e].index(s) + 1)

        def batches(eng, body):
            loops = (K - 3) // RING
            with eng.Fori(0, loops) as j:
                for u in range(RING):
                    body(Batch(j, u), K)
            for k in range(loops * RING, K):
                body(Batch(k // RING, k % RING), K - k)

        def block_regs(eng, tag):
            return [[eng.alloc_register(f"{tag}{u}_{i}") for i in range(B)] for u in range(RING)]

        MARKS = {}
        block = ctx.enter_context(nc.Block())

        @block.vector
        def _(dve):
            s_passed[dve] = sem("s_passed_dve")
            v = nc.vector
            seeded(dve, "hot sc1 sc2 sc3 sc top0 topf top ends0 ends1 ends2 runl runr rnew rdrop seg1 seg diff mask "
                        "resc mulv add prod dot tad h1 h2 h3 e1 e4 e5 e6 e7 e8 branch self2 sum stat aggr kept norm")
            regs = block_regs(dve, "blk_dve")
            step = [0]

            def ch(inst):
                step[0] += 1
                inst.then_inc(p_dve, 1)
                dve.wait_ge(p_dve, step[0])
                return step[0]

            def mark(name):
                MARKS[name] = step[0]

            def ones_cols(l):
                H, V, C = HEADS[l], COLS[l], CH[l]
                for u in range(2):
                    ch(v.memset(trow[:, u, 0:H * V].rearrange("p (h c) -> p h c", h=H)[:, :, C:V], 1.0))
            ones_cols(0)
            mark("ONES_DONE")

            def products(l):
                H = HEADS[l]
                dve.wait_ge(s_avec[l], 32)
                for i in range(2):
                    ch(v.tensor_tensor(wprod, wts[l][:, :, 0:D],
                                       avec[:, 2 * l + i, :].unsqueeze(1).to_broadcast([P, 2, D]), ALU.mult))
                    ch(v.tensor_reduce(wts[l][:, :, D + i * H:D + (i + 1) * H],
                                       wprod.rearrange("p c (h n) -> p c h n", h=H), AX.X, ALU.add))
            dve.wait_ge(s_w0, 16)
            products(0)
            mark("W0_DONE")
            dve.wait_ge(s_dst, 16)
            ch(v.tensor_copy(dst_allf, dst_all))
            for b in range(1, BLOCKS):
                ch(v.tensor_scalar(dead, dst_allf, float(P * b), 0.0, ALU.is_lt, ALU.add,
                                   accum_out=counts[:, b - 1:b]))
            mark("COUNT_DONE")
            dve.wait_ge(p_pe, 1)
            dve.wait_ge(p_pool, 13)
            off = misc[0:BLOCKS - 1, 1:2].bitcast(I32)
            shl = misc[0:BLOCKS - 1, 2:3].bitcast(I32)
            pos = misc[0:BLOCKS - 1, 3:4]
            ch(v.tensor_copy(off, ps_e[0:BLOCKS - 1, 0:1]))
            ch(v.tensor_scalar(shl, off, 7, None, ALU.logical_shift_right))
            ch(v.tensor_copy(pos, shl))
            ch(v.tensor_tensor(pos, pos, misc[0:BLOCKS - 1, 0:1], ALU.add))
            ch(v.tensor_scalar(slot_gt, siota, pos, None, ALU.is_gt))
            ch(v.tensor_scalar(slot_gt2, siota2, pos, None, ALU.is_gt))
            mark("GT_DONE")
            dve.wait_ge(p_pe, 6)
            ch(v.tensor_copy(blk[:, :], ps_T[0:1, 0:K * BPAD]))
            bcol = misc[0:Q, 8:12]
            b128 = misc[0:Q, 12:16]
            ch(v.tensor_copy(bcol, ps_hot[0:Q, 0:4]))
            ch(v.tensor_scalar(b128, bcol, float(P), None, ALU.mult))
            ch(v.tensor_tensor(misc[0:Q, 16:20].bitcast(I32), misc[0:Q, 4:8], bcol, ALU.subtract))
            mark("TILE_DONE")
            dve.wait_ge(s_w, 16 * 7)
            products(1)
            dve.wait_ge(s_got, 16 * 12)
            ch(v.tensor_copy(dstf.rearrange("p c e -> p (c e)"), dst_g))
            ch(v.tensor_copy(srcf.rearrange("p c e -> p (c e)"), src_g))
            for c in range(4):
                ch(v.tensor_scalar(loc_g[:, c, :], dstf[:, c, :], b128[:, c:c + 1], None, ALU.subtract))
            ch(v.tensor_copy(loc_b, loc_g.rearrange("p c e -> p (c e)")))
            mark("LOC_DONE")
            ch(v.tensor_scalar(key, loc_g, float(P), None, ALU.is_lt))
            ch(v.scalar_tensor_tensor(key, loc_g, 0.0, key, ALU.is_ge, ALU.mult))
            ch(v.scalar_tensor_tensor(key, dstf, 1.0, key, ALU.add, ALU.mult))
            ch(v.tensor_scalar(key, key, -1.0, None, ALU.add))
            mark("KEY_DONE")
            dve.wait_ge(s_near, 32)
            ch(v.tensor_tensor(flg[:, :, START, :], key, kprev, ALU.not_equal))
            ch(v.tensor_scalar(flg[:, :, PEN_F, :], flg[:, :, START, :], -BIG, None, ALU.mult))
            ch(v.tensor_tensor(flg[:, :, PEN_B, :], key, knext, ALU.not_equal))
            ch(v.tensor_scalar(flg[:, :, PEN_B, :], flg[:, :, PEN_B, :], -BIG, None, ALU.mult))
            for c in range(4):
                ch(v.tensor_scalar(flg[:, c, PEN_L, :], key[:, c, :], kprev[:, c, 0:1], -BIG,
                                   ALU.not_equal, ALU.mult))
                ch(v.tensor_scalar(flg[:, c, PEN_R, :], key[:, c, :], knext[:, c, P - 1:P], -BIG,
                                   ALU.not_equal, ALU.mult))
            one, cl, cr = misc[0:Q, 20:24], misc[0:Q, 24:28], misc[0:Q, 28:32]
            pab = misc[0:Q, 40:48].rearrange("p (t c) -> p t c", t=2)
            ch(v.tensor_tensor(one, key[:, :, 0], key[:, :, P - 1], ALU.is_equal))
            ch(v.tensor_tensor(cl, key[:, :, 0], kprev[:, :, 0], ALU.is_equal))
            ch(v.tensor_tensor(cr, key[:, :, P - 1], knext[:, :, P - 1], ALU.is_equal))
            for c in range(4):
                ch(v.tensor_scalar(car[:, c, :], iota[0:Q, :], loc_g[:, c, 0:1], cl[:, c:c + 1],
                                   ALU.is_equal, ALU.mult))
            ch(v.tensor_scalar(car1, car, -1.0, 1.0, ALU.mult, ALU.add))
            for i, w in enumerate((cl, cr)):
                ch(v.tensor_tensor(pab[:, i, :], w, one, ALU.mult))
                ch(v.tensor_scalar(pab[:, i, :], pab[:, i, :], -1.0, BIG, ALU.add, ALU.mult))
            mark("PREP_DONE")
            ch(v.tensor_copy(identb[:, :], ident[:, :]))
            ch(v.tensor_copy(pidx[:, :], misc[:, 0:1]))
            dve.wait_ge(p_pe, 10)
            ch(v.tensor_copy(index_all, bank[7][:, 0:SLOTS]))
            mark("INDEX_DONE")
            dve.wait_ge(p_pe, 14)
            for c in range(2):
                ch(v.tensor_copy(wts[2][:, c, 0:D], bank[0][:, c * D:(c + 1) * D]))
            products(2)
            mark("WA_DONE")
            parts = [attr_p[:, i, :, :, :].rearrange("p c j e -> p c e j") for i in range(3)]
            ch(v.tensor_copy(parts[0], attr_g))
            ch(v.tensor_tensor(attr_r, attr_g, parts[0], ALU.subtract))
            ch(v.tensor_copy(parts[1], attr_r))
            ch(v.tensor_tensor(parts[2], attr_r, parts[1], ALU.subtract))
            ch(v.tensor_copy(edgew_p[:, 0, :], edgew[:, :]))
            ch(v.tensor_tensor(edgewr[:, :], edgew[:, :], edgew_p[:, 0, :], ALU.subtract))
            ch(v.tensor_copy(edgew_p[:, 1, :], edgewr[:, :]))
            ch(v.tensor_tensor(edgew_p[:, 2, :], edgewr[:, :], edgew_p[:, 1, :], ALU.subtract))
            mark("PARTS_DONE")

            def stats_steps(first):
                def stat(b, u):
                    need_apart(dve, ("sum", first + b + 1))
                    done(v.bn_stats(stats[:, u, :], nodes[:, bass.ds(b, 1), :].rearrange("p a f -> p (a f)")), "stat")

                def aggregate(b, u):
                    need_apart(dve, ("stat", first + b + 1))
                    done(v.bn_aggr(mv[:, u, :], stats[:, u, :]), "aggr")

                def keep(b, u):
                    need(dve, "aggr", first + b + 1)
                    done(v.tensor_copy(meanvar[:, bass.ds(b, 1), :].rearrange("p a f -> p (a f)"), mv[:, u, :]),
                         "kept")
                return stat, aggregate, keep

            for l in range(3):
                H, C, V, VV = HEADS[l], CH[l], COLS[l], VALS[l]
                base = l * BLOCKS
                if l:
                    need(dve, "add", l * K * B)
                    for u in range(2):
                        dve.wait_ge(s_tab[l - 1][u], 16 * ((BLOCKS + 1 - u) // 2))
                    ones_cols(l)

                def weights_of_self(b, u):
                    Hh, Vh, W = HEADS[0], COLS[0], VALS[0]
                    a = sums[:, bass.ds(b * W, W)].rearrange("p (h c) -> p h c", h=Hh)
                    need(dve, "e2", b - 1)
                    done(v.scalar_tensor_tensor(small[:, u, 0, 0:Hh], a[:, :, Vh - 2], 0.0, a[:, :, Vh - 1],
                                                ALU.is_equal, ALU.add), "e1")

                def divide(b, u):
                    Hh, Vh, W = HEADS[0], COLS[0], VALS[0]
                    need(dve, "e3", b + 1)
                    t = work[:, u, 0:W].rearrange("p (h c) -> p h c", h=Hh)
                    done(v.reciprocal(small[:, u, 1, 0:Hh], t[:, :, Vh - 2]), "e4")
                    need(dve, "e4", b + 1)
                    need(dve, "e8", b - 1)
                    done(v.tensor_tensor(work2[:, u, :].rearrange("p (h c) -> p h c", h=Hh), t[:, :, 0:CH[0]],
                                         small[:, u, 1, 0:Hh].unsqueeze(2).to_broadcast([P, Hh, CH[0]]),
                                         ALU.mult), "e5")
                    need(dve, "e5", b + 1)
                    done(v.tensor_tensor(work2[:, u, :], work2[:, u, :], bias[:, 0, :], ALU.add), "e6")
                    need(dve, "e6", b + 1)
                    need(dve, "ex", b - 1)
                    done(v.tensor_scalar(work3[:, u, :], work2[:, u, :], 0.0, None, ALU.min), "e7")
                    done(v.tensor_scalar(work2[:, u, :], work2[:, u, :], 0.0, -1.0, ALU.max, ALU.add), "branch")

                def elu(b, u):
                    need(dve, "branch", b + 1)
                    need(dve, "ex", b + 1)
                    need(dve, "yTp", BLOCKS + b - 1)
                    done(v.tensor_tensor(yin[:, u, :], work2[:, u, :], expo[:, u, :], ALU.add), "e8")

                def h_part(b, i):
                    return hnode3[:, bass.ds(b, 1), i, :].rearrange("p a f -> p (a f)")

                def split1(b, u):
                    need(dve, "tval", 2 * BLOCKS + b + 1)
                    need(dve, "h3", b - 1)
                    h_ = trow[:, u, 0:VALS[2]].rearrange("p (h c) -> p h c", h=8)[:, :, 0:CH[2]]
                    done(v.tensor_tensor(work2[:, u, :].rearrange("p (h c) -> p h c", h=8), h_,
                                         h_part(b, 0).rearrange("p (h c) -> p h c", h=8), ALU.subtract), "h1")

                def split2(b, u):
                    need(dve, "h1", b + 1)
                    done(v.tensor_copy(h_part(b, 1), work2[:, u, :]), "h2")

                def split3(b, u):
                    need(dve, "h2", b + 1)
                    done(v.tensor_tensor(h_part(b, 2), work2[:, u, :], h_part(b, 1), ALU.subtract), "h3")

                def scores_out(l=l, H=H, base=base):
                    n = 2 * H if SELF[l] else H
                    need(dve, "tval", base + BLOCKS)
                    if l:
                        need(dve, "ad", l * K)
                    s_, d_ = (ntab[:, :, i * H:(i + 1) * H] for i in range(2))
                    if SELF[l]:
                        t, e_ = dtab[:, :, 0:H], dtab[:, :, H:n]
                        ch(v.tensor_tensor(t, s_, d_, ALU.add))
                        ch(v.scalar_tensor_tensor(e_, t, SLOPE, t, ALU.mult, ALU.max))
                    ch(v.tensor_copy(dtab[:, :, 0:H], d_))
                    for i in range(2):
                        ch(v.tensor_copy(dtab3[:, :, i, 0:n], dtab[:, :, 0:n]))
                        ch(v.tensor_tensor(dtab[:, :, 0:n], dtab[:, :, 0:n], dtab3[:, :, i, 0:n], ALU.subtract))
                    done(v.tensor_copy(dtab3[:, :, 2, 0:n], dtab[:, :, 0:n]), "tad")

                def self_loop(b, u):
                    a = sums[:, bass.ds(b * VALS[1], VALS[1])]
                    done(v.scalar_tensor_tensor(small[:, u, 0, 0:1], a[:, D:D + 1], 0.0, a[:, D + 1:D + 2],
                                                ALU.is_equal, ALU.add), "e1")

                def add_self(b, u):
                    a = sums[:, bass.ds(b * VALS[1], VALS[1])]
                    need(dve, "e1", BLOCKS + b + 1)
                    dve.wait_ge(s_self[1][u], (b - u) * 8 + 16)
                    done(v.scalar_tensor_tensor(work[:, u, 0:D + 1], self_row[:, u, 0:D + 1], small[:, u, 0, 0:1],
                                                a[:, 0:D + 1], ALU.mult, ALU.add), "self2")

                def invert(b, u):
                    need(dve, "self2", b + 1)
                    done(v.reciprocal(small[:, u, 1, 0:1], work[:, u, D:D + 1]), "e4")

                def residual(b, u):
                    need(dve, "e4", BLOCKS + b + 1)
                    y = nodes[:, bass.ds(b, 1), :].rearrange("p a f -> p (a f)")
                    done(v.scalar_tensor_tensor(y, work[:, u, 0:D], small[:, u, 1, 0:1], y, ALU.mult, ALU.add), "sum")

                def normalise(n, l_):
                    need(dve, "kept", l_ * BLOCKS)
                    ch(v.tensor_scalar(meanvar[:, :, 1], meanvar[:, :, 1], EPS, None, ALU.add))
                    v.sem_inc(s_layer, 1)
                    dve.wait_ge(p_act, n)
                    ch(v.reciprocal(rstd[:, :], rstd[:, :]))
                    for b in range(BLOCKS):
                        done(v.tensor_scalar(nodes[:, b, :], nodes[:, b, :], meanvar[:, b, 0:1], rstd[:, b:b + 1],
                                             ALU.subtract, ALU.mult), "norm")

                if l == 1:
                    staggered(dve, (weights_of_self, 2), (divide, 1), (elu, 0))
                elif l == 2:
                    dve.wait_ge(s_bias, 1)
                    twos(dve, self_loop, add_self, invert, residual, *stats_steps(0))
                    normalise(1, 1)
                    twos(dve, split1, split2, split3)
                scores_out()

                def hot(t, l=l):
                    kk = l * K + t.k
                    need(dve, "hotp", 2 * (kk - 2))
                    need(dve, "ad", kk - 2)
                    if l == 2:
                        need(dve, "encp", (t.k - 2) * B)
                    dve.wait_ge(s_meta[l][t.u], (t.j + 1) * (16 * META[l]))
                    done(v.tensor_scalar(onehotT[:, t.u, :], locb[:, t.u, :], pidx[:, :], None, ALU.is_equal), "hot")

                def scores(t, l=l, H=H, VV=VV):
                    kk = l * K + t.k
                    n = 2 * H if SELF[l] else H
                    sc = score[:, 0, 0:H * B].rearrange("p (h s) -> p s h", h=H)
                    ad = adsum[:, 0:n * B].rearrange("p (s n) -> p s n", s=B)
                    need(dve, "scT", kk)
                    need(dve, "ad", kk + 1)
                    need(dve, "w", kk)
                    done(v.tensor_reduce(ad, ps_e[:, AD:AD + 24 * B].rearrange("p (s i n) -> p s n i", s=B, i=3)[:, :, 0:n, :],
                                         AX.X, ALU.add), "sc1")
                    need(dve, "sc1", kk + 1)
                    dve.wait_ge(s_rows[l][t.u], (t.j + 1) * (16 * B))
                    if SELF[l]:
                        done(v.tensor_copy(score[:, 1, 0:H * B].rearrange("p (h s) -> p s h", h=H), ad[:, :, H:n]),
                             "sc2")
                        done(v.tensor_tensor(sc, rows[:, t.u, :, VV:VV + H], ad[:, :, 0:H], ALU.add), "sc3")
                    else:
                        done(v.tensor_tensor(sc, rows[:, t.u, :, VV:VV + H], ad[:, :, 0:H], ALU.add), "sc2")
                        need(dve, "dot", (t.k + 1) * B)
                        need(dve, "sc2", kk + 1)
                        done(v.tensor_tensor(sc, sc, dots[:, t.u, :, :], ALU.add), "sc3")
                    need(dve, "sc3", kk + 1)
                    s = score[:, 0, 0:H * B]
                    if SELF[l]:
                        need(dve, "sc2", kk + 1)
                    done(v.scalar_tensor_tensor(s, s, SLOPE, s, ALU.mult, ALU.max), "sc")

                def tops(t, l=l, H=H):
                    kk = l * K + t.k
                    R = H * B
                    need(dve, "scp", kk + 1)
                    dve.wait_ge(s_meta[l][t.u], (t.j + 1) * (16 * META[l]))
                    s0 = scoreT[0:R, 0, :]
                    if SELF[l]:
                        done(v.tensor_tensor(top[0:R, 0, :], s0, scoreT[0:R, 1, :], ALU.max), "top0")
                        need(dve, "top0", kk + 1)
                        s0 = top[0:R, 0, :]
                    done(v.tensor_tensor_scan(top[0:R, 1, :], flags[0:R, t.u, PEN_F, :], s0, -BIG,
                                              ALU.add, ALU.max), "topf")

                def tops2(t, l=l, H=H):
                    kk = l * K + t.k
                    R = H * B
                    need(dve, "topf", kk + 1)
                    need(dve, "endp", kk)
                    done(v.tensor_tensor_scan(top[0:R, 2, ::-1], flags[0:R, t.u, PEN_B, ::-1], top[0:R, 1, ::-1],
                                              -BIG, ALU.add, ALU.max), "top")

                def links(t, l=l, H=H):
                    kk = l * K + t.k
                    R = H * (B + 1)
                    e = [ends[0:1, i, 0:R].rearrange("p (h s) -> p h s", h=H) for i in range(2)]
                    r = [ps_row[:, i * 8 * B:i * 8 * B + H * B].rearrange("p (h s) -> p h s", h=H) for i in range(2)]
                    run = runs[0:1, 0, 0:R].rearrange("p (h s) -> p h s", h=H)
                    need(dve, "endp", kk + 1)
                    need(dve, "rdrop", kk)
                    done(v.tensor_copy(e[0][:, :, 1:], r[0]), "ends0")
                    done(v.tensor_copy(e[1][:, :, 0:B], r[1]), "ends1")
                    need(dve, "runl", kk)
                    done(v.tensor_copy(e[0][:, :, 0:1], run[:, :, B:B + 1]), "ends2")

                def links2(t, l=l, H=H):
                    kk = l * K + t.k
                    R = H * (B + 1)
                    need(dve, "ends2", kk + 1)
                    need(dve, "ends0", kk + 1)
                    need(dve, "ends1", kk + 1)
                    need(dve, "link", kk)
                    pen = [chain[0:1, t.u, i, 0:H, :].rearrange("p h s -> p (h s)") for i in range(2)]
                    done(v.tensor_tensor_scan(runs[0:1, 0, 0:R], pen[0], ends[0:1, 0, 0:R], -BIG,
                                              ALU.add, ALU.max), "runl")
                    done(v.tensor_tensor_scan(runs[0:1, 1, 0:R][:, ::-1], pen[1][:, ::-1], ends[0:1, 1, 0:R][:, ::-1],
                                              -BIG, ALU.add, ALU.max), "runr")
                    need(dve, "runr", kk + 1)
                    c = ends[0:1, 0, 0:R].rearrange("p (h s) -> p h s", h=H)[:, :, 0]
                    b = runs[0:1, 1, 0:R].rearrange("p (h s) -> p h s", h=H)[:, :, 0]
                    done(v.tensor_tensor(newtop[0:1, 0:H], c, b, ALU.max), "rnew")
                    need(dve, "rnew", kk + 1)
                    need(dve, "rscale", kk)
                    done(v.tensor_tensor(drop[0:1, 0:H], c, newtop[0:1, 0:H], ALU.subtract), "rdrop")

                def finish_tops(t, l=l, H=H):
                    kk = l * K + t.k
                    R = H * B
                    need(dve, "col", kk + 1)
                    done(v.scalar_tensor_tensor(seg[0:R, :], flags[0:R, t.u, PEN_L, :], ps_col[0:R, 0:1],
                                                top[0:R, 2, :], ALU.add, ALU.max), "seg1")
                    need(dve, "seg1", kk + 1)
                    done(v.scalar_tensor_tensor(seg[0:R, :], flags[0:R, t.u, PEN_R, :], ps_col[0:R, 1:2],
                                                seg[0:R, :], ALU.add, ALU.max), "seg")
                    need(dve, "seg", kk + 1)
                    need(dve, "wp", kk)
                    n = 2 if SELF[l] else 1
                    done(v.tensor_tensor(expT[0:R, 0:n, :], scoreT[0:R, 0:n, :],
                                         seg[0:R, :].unsqueeze(1).to_broadcast([R, n, P]), ALU.subtract), "diff")

                def mask(t, l=l, H=H):
                    kk = l * K + t.k
                    R = H * B
                    need(dve, "exp", kk + 1)
                    done(v.tensor_tensor(expT[0:R, 1, :], expT[0:R, 1, :], flags[0:R, t.u, START, :], ALU.mult),
                         "mask")

                def rescale(t, left, l=l, H=H, V=V, VV=VV):
                    kk = l * K + t.k
                    if left > 1:
                        need(dve, "ad", kk + 2)
                    need(dve, "fac", kk + 1)
                    need(dve, "w", kk + 1)
                    need(dve, "add", kk * B)
                    b = dve.snap(regs[t.u][0], min_val=0, max_val=BLOCKS - 1)
                    s = sums[:, bass.ds(b * VV, VV)].rearrange("p (h c) -> p h c", h=H)
                    done(v.tensor_tensor(s, s, ps_e[:, FAC:FAC + H].unsqueeze(2).to_broadcast([P, H, V]), ALU.mult),
                         "resc")

                def mul(t, s, l=l, H=H, V=V):
                    need(dve, "w", l * K + t.k + 1)
                    n = V - 1 if SELF[l] else V
                    r = rows[:, t.u, s, 0:H * V].rearrange("p (h c) -> p h c", h=H)[:, :, 0:n]
                    w = wgt[:, t.u, 0:H * B].rearrange("p (h s) -> p h s", h=H)[:, :, s:s + 1]
                    done(v.tensor_tensor(r, r, w.to_broadcast([P, H, n]), ALU.mult), "mulv")

                def add(t, s, l=l, VV=VV):
                    kk = l * K + t.k
                    b = dve.snap(regs[t.u][s], min_val=0, max_val=BLOCKS - 1)
                    a = sums[:, bass.ds(b * VV, VV)]
                    need(dve, "agg", kk * B + s + 1)
                    if s:
                        need(dve, "add", kk * B + s)
                    else:
                        need(dve, "resc", kk + 1)
                    done(v.tensor_tensor(a, a, ps_sum[l][s % len(ps_sum[l])][:, 0:VV], ALU.add), "add")

                def dot(t, s):
                    i = t.k * B + s
                    need(dve, "enc", i + 1)
                    done(v.tensor_tensor(prod[:, s % 3, :], prod[:, s % 3, :], ps_enc[s % 3][:, D:2 * D], ALU.mult),
                         "prod")

                def dot2(t, s):
                    i = t.k * B + s
                    need(dve, "prod", i + 1)
                    done(v.tensor_reduce(dots[:, t.u, s, :], prod[:, s % 3, :].rearrange("p (h c) -> p h c", h=8),
                                         AX.X, ALU.add), "dot")

                def load(t):
                    dve.load(regs[t.u], blk[0:1, bass.ds(t.k * BPAD, B)])

                def period(t, left, l=l):
                    n1, n2, n3 = t.after(1), t.after(2), t.after(3)
                    rescale(t, left)
                    for s in range(B):
                        if s + LEAD[l] in OWN[l]["V"]:
                            mul(t, s + LEAD[l])
                        if left > 1 and s + LEAD[l] - B in OWN[l]["V"]:
                            mul(n1, s + LEAD[l] - B)
                        if left > 3 and s == AT[l]["hot"]:
                            hot(n3)
                        enc = left > 3 and l == 2 and s >= AT[l]["encV"]
                        if enc:
                            dot(n3, s - AT[l]["encV"])
                        if left > 1:
                            if s == AT[l]["load"]:
                                load(n1)
                            if s == AT[l]["tops2"]:
                                tops2(n1)
                            if s == AT[l]["links"]:
                                links(n1)
                                links2(n1)
                            if s == AT[l]["finish"]:
                                finish_tops(n1)
                            if s == AT[l]["mask"] and SELF[l]:
                                mask(n1)
                        if left > 2:
                            if s == AT[l]["scores"]:
                                scores(n2)
                            if s == AT[l]["tops"]:
                                tops(n2)
                        add(t, s)
                        if enc:
                            dot2(n3, s - AT[l]["encV"])
                    if left > 3 and l == 2:
                        for s in range(B - AT[l]["encV"], B):
                            dot(n3, s)
                            dot2(n3, s)

                kk = l * K
                run = runs[0:1, 0, 0:H * (B + 1)].rearrange("p (h s) -> p h s", h=H)
                if l:
                    need(dve, "link", kk)
                ch(v.memset(runs[:, :, :], -BIG))
                if l:
                    need(dve, "rdrop", kk)
                    ch(v.memset(ends[:, :, :], -BIG))
                t0, t1, t2 = (Batch(0, k) for k in range(3))
                for t in (t0, t1, t2):
                    hot(t)
                if l == 2:
                    for t in (t0, t1, t2):
                        for s in range(B):
                            dot(t, s)
                            dot2(t, s)
                for f in (scores, tops, tops2, links, links2, finish_tops):
                    f(t0)
                if SELF[l]:
                    mask(t0)
                for s in range(LEAD[l]):
                    if s in OWN[l]["V"]:
                        mul(t0, s)
                scores(t1)
                tops(t1)
                if l == 0:
                    dve.wait_ge(s_flag, 16 * 6)
                    ch(v.memset(sums[:, :], 0.0))
                else:
                    dve.wait_ge(p_pool, 19 if l == 1 else 21)
                load(t0)
                batches(dve, period)

            def clamp(b, u):
                a = sums[:, bass.ds(b * VALS[2], VALS[2])].rearrange("p (h c) -> p h c", h=8)
                done(v.tensor_scalar(small[:, u, 0, :], a[:, :, CH[2]], 1e-10, None, ALU.max), "e1")

            def invert2(b, u):
                need(dve, "e1", 2 * BLOCKS + b + 1)
                done(v.reciprocal(small[:, u, 1, :], small[:, u, 0, :]), "e4")

            def scale2(b, u):
                a = sums[:, bass.ds(b * VALS[2], VALS[2])].rearrange("p (h c) -> p h c", h=8)
                need(dve, "e4", 2 * BLOCKS + b + 1)
                done(v.tensor_tensor(work2[:, u, :].rearrange("p (h c) -> p h c", h=8), a[:, :, 0:CH[2]],
                                     small[:, u, 1, :].unsqueeze(2).to_broadcast([P, 8, CH[2]]), ALU.mult), "e5")

            def residual2(b, u):
                need(dve, "e5", BLOCKS + b + 1)
                y = nodes[:, bass.ds(b, 1), :].rearrange("p a f -> p (a f)")
                done(v.tensor_tensor(y, y, work2[:, u, :], ALU.add), "sum")
            need(dve, "add", 3 * K * B)
            dve.wait_ge(s_bias, 2)
            twos(dve, clamp, invert2, scale2, residual2, *stats_steps(BLOCKS))
            normalise(2, 2)

        @block.sync
        def _(sp):
            s_passed[sp] = sem("s_passed_sp")
            sp.dma_start(dst_pad[0:E], dst).then_inc(s_dpad, 16)
            sp.dma_start(wts[0][:, :, 0:D], w1.rearrange("(c p) n -> p c n", p=P)).then_inc(s_w0, 16)
            for i, a in enumerate((as1, ad1)):
                sp.dma_start(avec[:, i, :], a.rearrange("h c -> (h c)").partition_broadcast(P)).then_inc(s_avec[0], 16)
            sp.wait_ge(p_pool, 5)
            left = TILES * P - E
            sp.dma_start(dst_pad[E:].rearrange("(a n) -> a n", a=1), tail_i[:, 0:left]).then_inc(s_dpad, 16)
            sp.dma_start(src_pad[0:E], src).then_inc(s_pad, 16)
            sp.dma_start(src_pad[E:].rearrange("(a n) -> a n", a=1), tail_i[:, P:P + left]).then_inc(s_pad, 16)
            sp.wait_ge(s_dpad, 32)
            sp.dma_start(dst_all, dst_pad.rearrange("(p t) -> p t", p=P)).then_inc(s_dst, 16)
            sp.dma_start(nodes[:, 0:FULL, :], x[0:FULL * P, :].rearrange("(b p) f -> p b f", p=P)).then_inc(s_in, 16)
            sp.dma_start(nodes[0:REST, FULL, :], x[FULL * P:N, :]).then_inc(s_in, 16)
            sp.dma_start(attr_pad[0:3 * E], edge_attr.rearrange("e j -> (e j)")).then_inc(s_pad, 16)
            sp.dma_start(attr_pad[3 * E:].rearrange("(a n) -> a n", a=1), tail_f[:, 0:3 * left]).then_inc(s_pad, 16)
            sp.dma_start(wts[1][:, :, 0:D], w2.rearrange("(c p) n -> p c n", p=P)).then_inc(s_w, 16)
            for l, pair in ((1, (as2, ad2)), (2, (as3, ad3))):
                for i, a in enumerate(pair):
                    sp.dma_start(avec[:, 2 * l + i, :], a.rearrange("h c -> (h c)").partition_broadcast(P)
                                 ).then_inc(s_avec[l], 16)
            sp.dma_start(w3in, w3.rearrange("(c p) n -> p c n", p=P)).then_inc(s_w, 16)
            with nc.allow_non_contiguous_dma(reason="768 words, once"):
                sp.dma_start(edgew[0:3, :], edge_w.rearrange("o j -> j o")).then_inc(s_w, 16)
            sp.dma_start(edgew[3:4, :], edge_b.rearrange("(a n) -> a n", a=1)).then_inc(s_w, 16)
            for l, b in enumerate((b1, b2, b3)):
                sp.dma_start(bias[:, l, :], b.partition_broadcast(P)).then_inc(s_w, 16)

            def edge_features():
                sp.wait_ge(p_dve, MARKS["PARTS_DONE"])
                for i in range(3):
                    for j in range(3):
                        sp.dma_start(attrT_d[3 * i + j, :].rearrange("(c q e) -> q c e", c=4, q=Q),
                                     attr_p[:, i, :, j, :]).then_inc(s_parts, 16)
                        sp.dma_start(edgew3[9 * i + 3 * j:9 * i + 3 * j + 3, :], edgew_p[0:3, i, :]
                                     ).then_inc(s_parts, 16)
                    sp.dma_start(edgew3[27 + i:28 + i, :], edgew_p[3:4, i, :]).then_inc(s_parts, 16)

            for l in range(3):
                H = HEADS[l]
                def write(b, u, l=l):
                    need_apart(sp, ("tval", l * BLOCKS + b + 1))
                    sp.dma_start(table[l][bass.ds(b * P, P), :], trow[:, u, 0:ROW[l]]).then_inc(s_tab[l][u], 16)

                if l:
                    need(sp, "add", l * K * B)
                    for u in range(2):
                        sp.wait_ge(s_tab[l - 1][u], 16 * ((BLOCKS + 1 - u) // 2))
                if l == 0:
                    pairs(sp, write)
                    sp.wait_ge(s_flag, 16 * 6)
                elif l == 1:
                    sp.dma_start(self_row[:, 0, 0:VALS[0]], table[0][0:P, 0:VALS[0]]).then_inc(s_self[0][0], 16)
                    sp.dma_start(self_row[:, 1, 0:VALS[0]], table[0][P:2 * P, 0:VALS[0]]).then_inc(s_self[0][1], 16)

                    def refill(b, u):
                        need_apart(sp, ("e2", b + 1))
                        sp.dma_start(self_row[:, u, 0:VALS[0]],
                                     table[0][bass.ds(b * P + 2 * P, P), 0:VALS[0]]).then_inc(s_self[0][u], 16)
                    for b in range(2):
                        refill(b, b)
                    with sp.Fori(0, (BLOCKS - 5) // 2) as j:
                        for u in range(2):
                            refill(j * 2 + (u + 2), u)
                            write(j * 2 + u, u)
                    refill(BLOCKS - 3, 0)
                    for b in range(BLOCKS - 5, BLOCKS):
                        write(b, b % 2)
                else:
                    need(sp, "e2", BLOCKS)
                    sp.dma_start(self_row[:, 0, 0:VALS[1]], table[1][0:P, 0:VALS[1]]).then_inc(s_self[1][0], 16)
                    sp.dma_start(self_row[:, 1, 0:VALS[1]], table[1][P:2 * P, 0:VALS[1]]).then_inc(s_self[1][1], 16)

                    def refill2(b, u):
                        need_apart(sp, ("self2", b + 1))
                        sp.dma_start(self_row[:, u, 0:VALS[1]],
                                     table[1][bass.ds(b * P + 2 * P, P), 0:VALS[1]]).then_inc(s_self[1][u], 16)
                    with sp.Fori(0, (BLOCKS - 3) // 2) as j:
                        for u in range(2):
                            refill2(j * 2 + u, u)
                    refill2(BLOCKS - 3, 0)
                    pairs(sp, write)

                def meta(t, l=l, H=H):
                    if not isinstance(t.j, int) or t.k >= RING:
                        need_apart(sp, ("fac", l * K + t.k - 2), ("hot", l * K + t.k - 2),
                                   ("mask" if SELF[l] else "diff", l * K + t.k - 2),
                                   (s_rows[l][t.u], t.j * (16 * B)))
                    sp.dma_start(index[:, t.u, :], index_d[bass.ds(t.k, 1), :, :].rearrange("a p s -> (a p) s")
                                 ).then_inc(s_index[l][t.u], 16)
                    for h in range(H):
                        sp.dma_start(flags[h * B:(h + 1) * B, t.u, :, :].rearrange("p t e -> p (t e)"),
                                     flags_d[bass.ds(t.k * B, B), :]).then_inc(s_meta[l][t.u], 16)
                    for i, at in ((0, 1), (1, 0)):
                        row = chain_d[i:i + 1, bass.ds(t.k * B, B)]
                        sp.dma_start(chain[0:1, t.u, i, 0:H, at:at + B],
                                     row.unsqueeze(1).to_broadcast([1, H, B])).then_inc(s_meta[l][t.u], 16)
                    sp.dma_start(carry[:, t.u, :], carry_d[bass.ds(t.k * B, 1), :, :].rearrange("a r e -> (a r) e")).then_inc(s_meta[l][t.u], 16)
                    sp.dma_start(locb[:, t.u, :], loc_d[bass.ds(t.k * B * P, B * P)].partition_broadcast(P)
                                 ).then_inc(s_meta[l][t.u], 16)
                    if l == 2:
                        for i in range(3):
                            sp.dma_start(attrT[9 * i:9 * i + 9, t.u, :],
                                         attrT_d[:, bass.ds(t.k * B * P, B * P)]).then_inc(s_meta[l][t.u], 16)

                if l == 2:
                    sp.wait_ge(p_pool, 20)
                for k in range(RING):
                    meta(Batch(0, k))
                if l == 0:
                    edge_features()
                with sp.Fori(1, K // RING) as j:
                    for u in range(RING):
                        meta(Batch(j, u))
                for k in range(K // RING * RING, K):
                    meta(Batch(k // RING, k % RING))
            for b in range(BLOCKS):
                n = P if b < FULL else REST
                need(sp, "norm", BLOCKS + b + 1)
                sp.dma_start(out[b * P:b * P + n, :], nodes[0:n, b, :]).then_inc(s_out, 16)
            sp.wait_ge(s_out, 16 * BLOCKS)

        @block.gpsimd
        def _(pool):
            s_passed[pool] = sem("s_passed_pool")
            g = nc.gpsimd
            seeded(pool, "e2 e3 mulp")
            g.memset(tail_i[:, 0:P], 100000).then_inc(p_pool, 1)
            g.memset(tail_i[:, P:2 * P], 0).then_inc(p_pool, 1)
            g.memset(tail_f[:, :], 0.0).then_inc(p_pool, 1)
            g.memset(nodes[:, FULL, :], 0.0).then_inc(p_pool, 1)
            g.memset(guard[:, :], -2.0).then_inc(p_pool, 1)
            g.memset(ident[:, :], 0.0).then_inc(p_pool, 1)
            g.iota(iota[:, :], [[1, P]], base=0, channel_multiplier=0,
                   allow_small_or_imprecise_dtypes=True).then_inc(p_pool, 1)
            g.iota(siota, [[B, K], [1, BPAD]], base=0, channel_multiplier=0,
                   allow_small_or_imprecise_dtypes=True).then_inc(p_pool, 1)
            g.iota(siota2, [[1, SLOTS]], base=0, channel_multiplier=0,
                   allow_small_or_imprecise_dtypes=True).then_inc(p_pool, 1)
            g.iota(misc[:, 0:1], [[0, 1]], base=0, channel_multiplier=1,
                   allow_small_or_imprecise_dtypes=True).then_inc(p_pool, 1)
            g.iota(misc[:, 4:8], [[Q, 4]], base=0, channel_multiplier=1,
                   allow_small_or_imprecise_dtypes=True).then_inc(p_pool, 1)
            g.memset(ones[:, :], 1.0).then_inc(p_pool, 1)
            g.memset(dtab3[:, :, :, :], 0.0).then_inc(p_pool, 1)
            pool.wait_ge(p_pool, 6)
            g.affine_select(out=ident[:, :], in_=ident[:, :], compare_op=ALU.not_equal, fill=1.0, base=0,
                            pattern=[[-1, P]], channel_multiplier=1).then_inc(p_pool, 1)
            g.memset(carry[:, :, :], 1.0).then_inc(p_pool, 1)
            g.memset(scale[:, :], 1.0).then_inc(p_pool, 1)
            g.memset(chain[:, :, :, :, :], -BIG).then_inc(p_pool, 1)
            g.memset(ends[:, :, :], -BIG).then_inc(p_pool, 1)
            pool.wait_ge(p_dve, MARKS["TILE_DONE"])
            pool.wait_ge(s_dpad, 32)
            pool.wait_ge(s_pad, 64)
            tcol = misc[:, 16:20].bitcast(I32)
            for c in range(4):
                for to, frm in ((dst_g[:, c * P:(c + 1) * P], dst_pad.rearrange("(t e) -> t e", e=P)),
                                (src_g[:, c * P:(c + 1) * P], src_pad.rearrange("(t e) -> t e", e=P)),
                                (attr_g[:, c, :, :].rearrange("p e j -> p (e j)"),
                                 attr_pad.rearrange("(t e) -> t e", e=3 * P))):
                    g.indirect_dma_start(out=to, out_offset=None, in_=frm,
                                         in_offset=bass.IndirectOffsetOnAxis(ap=tcol[0:Q, c:c + 1], axis=0)
                                         ).then_inc(s_got, 16)
            pool.wait_ge(p_dve, MARKS["KEY_DONE"])
            g.dma_start(keys_d[1:1 + SLOTS * P].rearrange("(c q e) -> q c e", c=4, q=Q), key).then_inc(s_key, 16)
            g.dma_start(keys_d[0:1].rearrange("(a n) -> a n", a=1), guard[:, 0:1]).then_inc(s_key, 16)
            g.dma_start(keys_d[SLOTS * P + 1:].rearrange("(a n) -> a n", a=1), guard[:, 1:2]).then_inc(s_key, 16)
            pool.wait_ge(s_key, 48)
            g.dma_start(kprev, keys_d[0:SLOTS * P].rearrange("(c q e) -> q c e", c=4, q=Q)).then_inc(s_near, 16)
            g.dma_start(knext, keys_d[2:].rearrange("(c q e) -> q c e", c=4, q=Q)).then_inc(s_near, 16)
            pool.wait_ge(p_dve, MARKS["PREP_DONE"])
            with nc.allow_non_contiguous_dma(reason="short runs, once"):
                g.dma_start(chain_d.rearrange("t (c q) -> q t c", c=4),
                            misc[0:Q, 40:48].rearrange("p (t c) -> p t c", t=2)).then_inc(s_flag, 16)
            g.dma_start(flags_d.rearrange("(c q) f -> q c f", c=4),
                        flg.rearrange("p c t e -> p c (t e)")).then_inc(s_flag, 16)
            for i, v in enumerate((car, car1)):
                g.dma_start(carry_d[:, i, :].rearrange("(c q) e -> q c e", c=4), v).then_inc(s_flag, 16)
            g.dma_start(loc_d.rearrange("(c q e) -> q c e", c=4, q=Q),
                        loc_b.rearrange("p (c e) -> p c e", c=4)).then_inc(s_flag, 16)
            pool.wait_ge(p_dve, MARKS["INDEX_DONE"])
            with nc.allow_non_contiguous_dma(reason="short runs, once"):
                g.dma_start(index_d.rearrange("k p s -> p k s"),
                            index_all.rearrange("p (k s) -> p k s", k=K)).then_inc(s_flag, 16)

            for l in range(3):
                base = l * BLOCKS
                if l == 2:
                    pool.wait_ge(s_parts, 16 * 21)
                    g.memset(attrT[:, :, :], 1.0).then_inc(p_pool, 1)
                if l == 1:
                    def selfs(b, u):
                        H, C, V = HEADS[0], COLS[0], VALS[0]
                        q = small[:, u, 0, 0:H]
                        need(pool, "e1", b + 1)
                        pool.wait_ge(s_self[0][u], (b - u) * 8 + 16)
                        need(pool, "e5", b - 1)
                        t = work[:, u, 0:V].rearrange("p (h c) -> p h c", h=H)[:, :, 0:C - 1]
                        r = self_row[:, u, 0:V].rearrange("p (h c) -> p h c", h=H)[:, :, 0:C - 1]
                        a = sums[:, bass.ds(b * V, V)].rearrange("p (h c) -> p h c", h=H)[:, :, 0:C - 1]
                        done(g.tensor_tensor(t, r, q.unsqueeze(2).to_broadcast([P, H, C - 1]), ALU.mult), "e2")
                        need(pool, "e2", b + 1)
                        done(g.tensor_tensor(t, t, a, ALU.add), "e3")
                    with pool.Fori(0, BLOCKS // 2) as j:
                        selfs(j * 2, 0)
                        selfs(j * 2 + 1, 1)
                    selfs(BLOCKS - 1, 0)
                if l:
                    need(pool, "e3" if l == 1 else "self2", BLOCKS)
                    g.memset(sums[:, :], 0.0).then_inc(p_pool, 1)
                if l == 0:
                    pool.wait_ge(p_dve, MARKS["WA_DONE"])
                need(pool, "tad", l + 1)
                for u in range(2):
                    pool.wait_ge(s_tab[l][u], 16 * ((BLOCKS + 1 - u) // 2))

                def gather(t, l=l):
                    old = not isinstance(t.j, int) or t.k >= RING
                    if old:
                        need_apart(pool, (s_index[l][t.u], t.j * 16 + 16))
                    else:
                        pool.wait_ge(s_index[l][t.u], t.j * 16 + 16)
                    for lo, hi in GATHERS:
                        if old:
                            need_apart(pool, ("agg", (t.k + (l * K - 3)) * B + hi))
                        for s in range(lo, hi):
                            g.indirect_dma_start(out=rows[:, t.u, s, 0:ROW[l]], out_offset=None, in_=table[l],
                                                 in_offset=bass.IndirectOffsetOnAxis(ap=index[:, t.u, s:s + 1], axis=0)
                                                 ).then_inc(s_rows[l][t.u], 16)
                for k in range(RING):
                    gather(Batch(0, k))

                def mul(t, s, l=l):
                    H, V = HEADS[l], COLS[l]
                    n = V - 1 if SELF[l] else V
                    need(pool, "w", l * K + t.k + 1)
                    r = rows[:, t.u, s, 0:H * V].rearrange("p (h c) -> p h c", h=H)[:, :, 0:n]
                    w = wgt[:, t.u, 0:H * B].rearrange("p (h s) -> p h s", h=H)[:, :, s:s + 1]
                    done(g.tensor_tensor(r, r, w.to_broadcast([P, H, n]), ALU.mult), "mulp")

                def period(t, left, l=l):
                    for s in OWN[l]["P"]:
                        mul(t, s)
                    if left > 3:
                        gather(t.after(3))
                batches(pool, period)
                if l != 1:
                    need(pool, "ycopy", BLOCKS if l == 0 else 2 * BLOCKS)
                    g.tensor_tensor(nodes[:, :, :], nodes[:, :, :],
                                    bias[:, 1 if l == 0 else 2, :].unsqueeze(1).to_broadcast([P, BLOCKS, D]), ALU.add
                                    ).then_inc(s_bias, 1)

        @block.scalar
        def _(act):
            s_passed[act] = sem("s_passed_act")
            a = nc.scalar
            seeded(act, "link hotT scp rscale exp w mula enc ycopy yT tval ex")
            for l in range(3):
                H, C, V = HEADS[l], CH[l], COLS[l]
                base = l * BLOCKS

                def take(b, u, l=l, base=base):
                    if l != 1:
                        need(act, "yTp", base + b - 1)
                        if l == 2:
                            need(act, "norm", b + 1)
                        else:
                            act.wait_ge(s_in, 32)
                        done(a.copy(yin[:, u, :], nodes[:, bass.ds(b, 1), :].rearrange("p a f -> p (a f)")), "ycopy")
                    else:
                        need(act, "e7", b + 1)
                        need(act, "e8", b - 1)
                        done(a.activation(expo[:, u, :], work3[:, u, :], ACT.Exp), "ex")

                def turned(b, u, base=base):
                    need(act, "yp", base + b - 1)
                    need(act, "yTp", base + b + 1)
                    done(a.copy(yT[:, u, :, :].rearrange("p c n -> p (c n)"), ps_yT[u][:, 0:2 * P]), "yT")

                def store(b, u, l=l, H=H, C=C, V=V, base=base):
                    need(act, "yp", base + b + 1)
                    free(act, s_tab[l][u], b, u)
                    a.copy(ntab[:, bass.ds(b, 1), 0:2 * H].rearrange("p a n -> p (a n)"), ps_y[u][:, D:D + 2 * H])
                    a.copy(trow[:, u, H * V:H * V + H], ps_y[u][:, D:D + H])
                    if l == 2:
                        need(act, "h1", b - 1)
                        a.copy(hnode3[:, bass.ds(b, 1), 0, :].rearrange("p a f -> p (a f)"), ps_y[u][:, 0:D])
                    done(a.copy(trow[:, u, 0:H * V].rearrange("p (h c) -> p h c", h=H)[:, :, 0:C],
                                ps_y[u][:, 0:D].rearrange("p (h c) -> p h c", h=H)), "tval")

                act.wait_ge(p_pool, 13)
                if l == 2:
                    act.wait_ge(s_flag, 16 * 6)
                    act.wait_ge(s_parts, 16 * 21)
                if l == 0:
                    act.wait_ge(p_dve, MARKS["ONES_DONE"])
                if l == 2:
                    act.wait_ge(s_layer, 1)
                    a.activation(rstd[:, :], meanvar[:, :, 1], ACT.Sqrt).then_inc(p_act, 1)
                if l == 1:
                    staggered(act, (take, 2), (turned, 1), (store, 0))
                else:
                    staggered(act, (turned, 1), (take, 2), (store, 0))

                def hotT(t, g, l=l):
                    kk = l * K + t.k
                    lo, hi = HOTS[g]
                    need(act, "hotp", 2 * kk + g + 1)
                    need(act, "agg", (kk - 2) * B)
                    done(a.copy(onehot[:, t.u, lo:hi, :].rearrange("p s e -> p (s e)"),
                                ps_hotb[l][g][:, 0:(hi - lo) * P]), "hotT")

                def scores(t, l=l, H=H):
                    kk = l * K + t.k
                    n = 2 if SELF[l] else 1
                    need(act, "scT", kk + 1)
                    done(a.copy(scoreT[0:H * B, 0:n, :].rearrange("p a e -> p (a e)"),
                                ps_T[0:H * B, 0:n * P]), "scp")

                def link(t, l=l, H=H):
                    kk = l * K + t.k
                    need(act, "runr", kk + 1)
                    need(act, "col", kk)
                    for i in range(2):
                        r = a.copy(linkrow[0:1, i, 0:H * B].rearrange("p (h s) -> p h s", h=H),
                                   runs[0:1, i, 0:H * (B + 1)].rearrange("p (h s) -> p h s", h=H)[:, :, i:i + B])
                    done(r, "link")

                def rescale(t, l=l, H=H):
                    kk = l * K + t.k
                    need(act, "rdrop", kk + 1)
                    need(act, "fac", kk)
                    done(a.activation(scale[0:1, 0:H], drop[0:1, 0:H], ACT.Exp), "rscale")

                def expw(t, l=l, H=H):
                    kk = l * K + t.k
                    n = 2 if SELF[l] else 1
                    need(act, "diff", kk + 1)
                    done(a.activation(expT[0:H * B, 0:n, :], expT[0:H * B, 0:n, :], ACT.Exp), "exp")

                def weights(t, l=l, H=H, V=V):
                    kk = l * K + t.k
                    need(act, "wp", kk + 1)
                    if SELF[l]:
                        a.copy(rows[:, t.u, :, 0:H * V].rearrange("p s (h c) -> p h s c", h=H)[:, :, :, V - 1],
                               ps_e[:, QT:QT + H * B].rearrange("p (h s) -> p h s", h=H))
                    done(a.copy(wgt[:, t.u, 0:H * B], ps_e[:, WT:WT + H * B]), "w")

                def mul(t, s, l=l, H=H, V=V):
                    need(act, "w", l * K + t.k + 1)
                    n = V - 1 if SELF[l] else V
                    for h in range(H):
                        r = rows[:, t.u, s, h * V:h * V + n]
                        i = a.activation(r, r, ACT.Copy, scale=wgt[:, t.u, h * B + s:h * B + s + 1])
                    done(i, "mula")

                def encode(t, s):
                    i = t.k * B + s
                    need(act, "encp", i + 1)
                    need(act, "dot", i - 1 if s < 2 else i - 2)
                    done(a.activation(prod[:, s % 3, :], ps_enc[s % 3][:, 0:D], ACT.Relu), "enc")

                def period(t, left, l=l):
                    n1, n2, n3 = t.after(1), t.after(2), t.after(3)
                    for s in range(B):
                        if left > 3 and l == 2 and s >= AT[l]["encA"]:
                            encode(n3, s - AT[l]["encA"])
                        if s + LEAD[l] in OWN[l]["A"]:
                            mul(t, s + LEAD[l])
                        if left > 1:
                            if s == AT[l]["link"]:
                                link(n1)
                                rescale(n1)
                            if s == AT[l]["exp"]:
                                expw(n1)
                            if s == AT[l]["weights"]:
                                weights(n1)
                            if s + LEAD[l] - B in OWN[l]["A"]:
                                mul(n1, s + LEAD[l] - B)
                        if left > 2 and s in (AT[l]["hotT"], AT[l]["hotT"] + 1):
                            hotT(n2, s - AT[l]["hotT"])
                        if left > 2 and s == AT[l]["copy"]:
                            scores(n2)
                    if left > 3 and l == 2:
                        for s in range(B - AT[l]["encA"], B):
                            encode(n3, s)

                t0, t1, t2 = (Batch(0, k) for k in range(3))
                for t in (t0, t1):
                    for g in range(2):
                        hotT(t, g)
                if l == 2:
                    for t in (t0, t1, t2):
                        for s in range(B):
                            encode(t, s)
                for f in (scores, link, rescale, expw, weights):
                    f(t0)
                for s in range(LEAD[l]):
                    if s in OWN[l]["A"]:
                        mul(t0, s)
                scores(t1)
                batches(act, period)
            act.wait_ge(s_layer, 2)
            a.activation(rstd[:, :], meanvar[:, :, 1], ACT.Sqrt).then_inc(p_act, 1)

        @block.tensor
        def _(pe):
            s_passed[pe] = sem("s_passed_pe")
            m = nc.tensor
            seeded(pe, "hotp ad scT endp fac col wp agg encp yTp yp")
            regs = block_regs(pe, "blk_pe")
            pe.wait_ge(p_pool, 18)
            pe.wait_ge(p_dve, MARKS["COUNT_DONE"])
            m.matmul(ps_e[0:BLOCKS - 1, 0:1], counts, ones[:, :], start=True, stop=True).then_inc(p_pe, 1)
            pe.wait_ge(p_dve, MARKS["GT_DONE"])
            m.matmul(ps_T[0:1, 0:K * BPAD], ones[0:BLOCKS - 1, :], slot_gt, start=True, stop=True).then_inc(p_pe, 1)
            for c in range(4):
                m.matmul(ps_hot[0:Q, c:c + 1], slot_gt2[:, c * Q:(c + 1) * Q], ones[0:BLOCKS - 1, :],
                         start=True, stop=True).then_inc(p_pe, 1)

            def transposes():
                pe.wait_ge(p_dve, MARKS["LOC_DONE"])
                for c in range(4):
                    m.transpose(bank[7][:, c * Q:(c + 1) * Q], srcf[:, c, :], ident[0:Q, 0:Q]).then_inc(p_pe, 1)
                pe.wait_ge(s_w, 16 * 7)
                for c in range(2):
                    for o in range(2):
                        m.transpose(bank[0][:, c * D + o * P:c * D + (o + 1) * P], w3in[:, o, c * P:(c + 1) * P],
                                    ident[:, :]).then_inc(p_pe, 1)

            for l in range(3):
                H, C, V, VV = HEADS[l], CH[l], COLS[l], VALS[l]
                base = l * BLOCKS

                def turn(b, u, l=l, base=base):
                    need(pe, "ycopy" if l != 1 else "e8", base + b + 1 if l == 0 else (b + 1 if l == 1 else BLOCKS + b + 1))
                    need(pe, "yT", base + b - 1)
                    for c in range(2):
                        i = m.transpose(ps_yT[u][:, c * P:(c + 1) * P], yin[:, u, c * P:(c + 1) * P], ident[:, :])
                    done(i, "yTp")

                def project(b, u, l=l, H=H, base=base):
                    need(pe, "yT", base + b + 1)
                    need(pe, "tval", base + b - 1)
                    for c in range(2):
                        i = m.matmul(ps_y[u][:, 0:D + 2 * H], yT[:, u, c, :], wts[l][:, c, :],
                                     start=(c == 0), stop=(c == 1))
                    done(i, "yp")

                if l == 0:
                    pe.wait_ge(p_dve, MARKS["W0_DONE"])
                staggered(pe, (turn, 1), (project, 0))
                if l == 0:
                    transposes()
                    pe.wait_ge(p_dve, MARKS["WA_DONE"])

                def hot(t, g, l=l):
                    kk = l * K + t.k
                    if g == 0:
                        need(pe, "hot", kk + 1)
                    need(pe, "hotT", 2 * kk + g - (1 if l < 2 else 0))
                    lo, hi = HOTS[g]
                    for s in range(lo, hi):
                        r = m.transpose(ps_hotb[l][g][:, (s - lo) * P:(s - lo + 1) * P], onehotT[:, t.u, s * P:(s + 1) * P],
                                        identb[:, :])
                    done(r, "hotp")

                def adst(t, l=l, H=H):
                    kk = l * K + t.k
                    need(pe, "hot", kk + 1)
                    need(pe, "w", kk - 1)
                    need(pe, "resc", kk - 1)
                    need(pe, "sc1", kk)
                    for s in range(B):
                        b = pe.snap(regs[t.u][s], min_val=0, max_val=BLOCKS - 1)
                        r = m.matmul(ps_e[:, AD + s * 24:AD + (s + 1) * 24], onehotT[:, t.u, s * P:(s + 1) * P],
                                     dtab3[:, bass.ds(b, 1), :, :].rearrange("p a i n -> p (a i n)"),
                                     start=True, stop=True)
                    done(r, "ad")

                def scoresT(t, l=l, H=H):
                    kk = l * K + t.k
                    need_apart(pe, ("sc", kk + 1), ("diff", kk))
                    for i in range(2 if SELF[l] else 1):
                        r = m.transpose(ps_T[0:H * B, i * P:(i + 1) * P], score[:, i, 0:H * B], ident[:, :])
                    done(r, "scT")

                def endsT(t, l=l, H=H):
                    kk = l * K + t.k
                    need_apart(pe, ("top", kk + 1))
                    for i, e in enumerate((P - 1, 0)):
                        r = m.transpose(ps_row[:, i * 8 * B:i * 8 * B + H * B], top[0:H * B, 2, e:e + 1],
                                        ident[0:H * B, 0:H * B])
                    done(r, "endp")

                def cols(t, l=l, H=H):
                    kk = l * K + t.k
                    need_apart(pe, ("link", kk + 1))
                    for i in range(2):
                        r = m.matmul(ps_col[0:H * B, i:i + 1], linkrow[0:1, i, 0:H * B], ones[0:1, :], start=True, stop=True)
                    done(r, "col")

                def factor(t, l=l, H=H):
                    kk = l * K + t.k
                    need(pe, "rscale", kk + 1)
                    need(pe, "resc", kk)
                    need(pe, "w", kk)
                    need(pe, "sc1", kk + 1)
                    m.matmul(ps_e[:, FAC:FAC + H], carry[:, t.u, :], scale[:, 0:H],
                             start=True, stop=True).then_inc(ev["fac"], 1)

                def weightsT(t, l=l, H=H):
                    kk = l * K + t.k
                    need_apart(pe, ("exp", kk + 1), ("w", kk))
                    m_ = m.transpose(ps_e[:, WT:WT + H * B], expT[0:H * B, 0, :], ident[0:H * B, 0:H * B])
                    if SELF[l]:
                        need_apart(pe, ("mask", kk + 1))
                        m_ = m.transpose(ps_e[:, QT:QT + H * B], expT[0:H * B, 1, :], ident[0:H * B, 0:H * B])
                    done(m_, "wp")

                def sum_slot(t, s, l=l, VV=VV):
                    i = (l * K + t.k) * B + s
                    nb = len(ps_sum[l])
                    if s == 0:
                        need(pe, "hotT", 2 * (l * K + t.k) + 2)
                    weighted(pe, l, t.k, s)
                    need(pe, "add", (l * K + t.k) * B + (s - nb + 1 if s >= nb else 0))
                    done(m.matmul(ps_sum[l][s % nb][:, 0:VV], onehot[:, t.u, s, :], rows[:, t.u, s, 0:VV],
                                  start=True, stop=True), "agg")

                def encode(t, s):
                    i = t.k * B + s
                    need(pe, "prod", i - 1 if s < 2 else i - 2)
                    if s == 0:
                        pe.wait_ge(s_meta[2][t.u], (t.j + 1) * 16 * META[2])
                        need(pe, "hot", 2 * K + t.k + 1)
                    p = ps_enc[s % 3]
                    m.matmul(p[:, 0:D], attrT[:, t.u, s * P:(s + 1) * P], edgew3[:, :], start=True, stop=True)
                    b = pe.snap(regs[t.u][s], min_val=0, max_val=BLOCKS - 1)
                    for i in range(3):
                        r = m.matmul(p[:, D:2 * D], onehotT[:, t.u, s * P:(s + 1) * P],
                                     hnode3[:, bass.ds(b, 1), i, :].rearrange("p a f -> p (a f)"),
                                     start=(i == 0), stop=(i == 2))
                    done(r, "encp")

                def load(t):
                    pe.load(regs[t.u], blk[0:1, bass.ds(t.k * BPAD, B)])

                def period(t, left, l=l):
                    n1, n2, n3 = t.after(1), t.after(2), t.after(3)
                    if left > 3:
                        load(n3)
                    for s in range(B):
                        if left > 3 and l == 2 and s >= AT[l]["encP"]:
                            encode(n3, s - AT[l]["encP"])
                        sum_slot(t, s)
                        if left > 1:
                            if s == AT[l]["endsT"]:
                                endsT(n1)
                            if s == AT[l]["cols"]:
                                cols(n1)
                                factor(n1)
                            if s == AT[l]["weightsT"]:
                                weightsT(n1)
                        if left > 2:
                            if s in (AT[l]["hotP"], AT[l]["hotP"] + 1):
                                hot(n2, s - AT[l]["hotP"])
                            if s == AT[l]["adst"]:
                                adst(n2)
                            if s == AT[l]["scoresT"]:
                                scoresT(n2)
                    if left > 3 and l == 2:
                        for s in range(B - AT[l]["encP"], B):
                            encode(n3, s)

                need(pe, "tad", l + 1)
                if l == 2:
                    need(pe, "h3", BLOCKS)
                    pe.wait_ge(s_parts, 16 * 21)
                t0, t1, t2 = (Batch(0, k) for k in range(3))
                for t in (t0, t1):
                    for g in range(2):
                        hot(t, g)
                for t in (t0, t1, t2):
                    load(t)
                    if l == 2:
                        for s in range(B):
                            encode(t, s)
                adst(t0)
                for f in (scoresT, endsT, cols, factor):
                    f(t0)
                adst(t1)
                weightsT(t0)
                scoresT(t1)
                batches(pe, period)


_INS = ("x", "src", "dst", "edge_attr_3", "L0_gnn_W1", "L0_gnn_a_src1", "L0_gnn_a_dst1", "L0_gnn_b1", "L0_gnn_W2",
        "L0_gnn_a_src2", "L0_gnn_a_dst2", "L0_gnn_b2", "L1_gnn_W", "L1_gnn_a_src", "L1_gnn_a_dst", "L1_gnn_edge_W",
        "L1_gnn_edge_b", "L1_gnn_bias")


def kernel(**inputs):
    import numpy as np
    import concourse.bacc as bacc
    from concourse.bass_utils import run_bass_kernel_spmd

    nc = bacc.Bacc("TRN2", target_bir_lowering=False, num_devices=1)
    arrays, args = {}, []
    for name in _INS:
        a = np.ascontiguousarray(inputs[name])
        arrays[f"in_{name}"] = a
        args.append(nc.dram_tensor(f"in_{name}", a.shape, mybir.dt.from_np(a.dtype), kind="ExternalInput").ap())
    out = nc.dram_tensor("out", (N, D), F32, kind="ExternalOutput").ap()
    gat_kernel(nc, *args, out)
    r = run_bass_kernel_spmd(nc, [arrays], core_ids=[0])
    return r.results[0]["out"]
```
